# Optimizing a Trainium2 kernel written in Bass

```python
import numpy as np
import jax
import jax.numpy as jnp

def _softmax(x, axis=-1):
    return jax.nn.softmax(x, axis=axis)

def _gelu(x):
    return jax.nn.gelu(x, approximate=True)

def _silu(x):
    return jax.nn.silu(x)

def _sigmoid(x):
    return jax.nn.sigmoid(x)

def _layernorm(x, axis=-1, eps=1e-05):
    m = jnp.mean(x, axis=axis, keepdims=True)
    v = jnp.var(x, axis=axis, keepdims=True)
    return (x - m) / jnp.sqrt(v + eps)

def _scatter_add(tgt, idx, src, axis=0):
    return tgt.at[idx].add(src)

def _segment_sum(src, seg, n):
    return jax.ops.segment_sum(src, seg, n)
kernel_name = 'mk_adj_preln_d2_adj_r2_3b3858'

def setup_inputs(seed: int=0):
    np.random.seed(seed)
    _w = jnp.asarray

    def _rec_inputs():
        import jax
        import jax.numpy as jnp
        _gk = jax.random.key(seed)
        x = 7.22e-05 + 1 * jax.random.normal(jax.random.fold_in(_gk, 1), (32, 256, 256), jnp.float32)
        _w = (1.0 + jnp.arange(256, dtype=jnp.float32)) ** (-0.5)
        _w = _w / _w.mean()
        _pij = jnp.clip(0.0078125 * _w[:, None] * _w[None, :], 0.0, 1.0)
        _a = jax.random.uniform(jax.random.fold_in(_gk, 2), (256, 256)) < _pij
        adj = _a.astype(jnp.int32)
        return (x, adj)
    x, adj = _rec_inputs()

    def _L0_gnn_setup():
        import jax, jax.numpy as jnp
        import numpy as np
        LEAKY_ALPHA = 0.01
        NEG_INF = -1000000000.0
        LN_EPS = 1e-05

        def _gat_heads(x, adj, W, a):
            O = W.shape[-1]
            Wh = jnp.einsum('bnf,hfo->bhno', x, W)
            f1 = jnp.einsum('bhno,ho->bhn', Wh, a[:, :O])
            f2 = jnp.einsum('bhno,ho->bhn', Wh, a[:, O:])
            e = f1[:, :, :, None] + f2[:, :, None, :]
            e = jnp.where(e > 0, e, LEAKY_ALPHA * e)
            e = jnp.where(adj[None, None] > 0, e, NEG_INF)
            attn = jax.nn.softmax(e, axis=-1)
            return jnp.einsum('bhnm,bhmo->bhno', attn, Wh)
        key = jax.random.key(seed)
        ks = jax.random.split(key, 10)
        B, N, F_in, F_hid, H, F_out, D_ff = (8, 1024, 256, 256, 4, 256, 256)
        s = 0.05
        return {'enc_inputs': jax.random.normal(ks[0], (B, N, F_in), jnp.float32), 'adj': jax.random.randint(ks[1], (N, N), 0, 2, jnp.int32), 'W_heads': jax.random.normal(ks[2], (H, F_in, F_hid), jnp.float32) * s, 'a_heads': jax.random.normal(ks[3], (H, 2 * F_hid), jnp.float32) * s, 'W_out': jax.random.normal(ks[4], (H * F_hid, F_out), jnp.float32) * s, 'a_out': jax.random.normal(ks[5], (2 * F_out,), jnp.float32) * s, 'w1': jax.random.normal(ks[6], (F_out, D_ff), jnp.float32) * s, 'b1': jnp.zeros((D_ff,), jnp.float32), 'w2': jax.random.normal(ks[7], (D_ff, F_out), jnp.float32) * s, 'b2': jnp.zeros((F_out,), jnp.float32), 'ln_gamma': jnp.ones((F_out,), jnp.float32), 'ln_beta': jnp.zeros((F_out,), jnp.float32)}
    _L0_gnn_all = _L0_gnn_setup()
    _L0_gnn_in = {k: v for k, v in _L0_gnn_all.items() if k in ('W_heads', 'a_heads', 'W_out', 'a_out', 'w1', 'b1', 'w2', 'b2', 'ln_gamma', 'ln_beta')}
    del _L0_gnn_all

    def _L1_gnn_setup():
        import jax, jax.numpy as jnp
        import numpy as np
        B, N, F, F1 = (512, 75, 256, 128)
        NEG = -1000000000.0
        ALPHA = 0.2
        key = jax.random.key(seed)
        k1, k2, k3, k4 = jax.random.split(key, 4)
        X = jax.random.normal(k1, (B, N, F), dtype=jnp.float32)
        A = jax.random.randint(k2, (N, N), 0, 2, dtype=jnp.int32)
        W = jax.random.normal(k3, (F, F1), dtype=jnp.float32) * (1.0 / np.sqrt(F))
        a = jax.random.normal(k4, (2, F1, 1), dtype=jnp.float32) * (1.0 / np.sqrt(F1))
        return {'X': X, 'A': A, 'W': W, 'a': a}
    _L1_gnn_all = _L1_gnn_setup()
    _L1_gnn_in = {k: v for k, v in _L1_gnn_all.items() if k in ('W', 'a')}
    del _L1_gnn_all
    return {'x': x, 'adj': adj, 'L0_gnn_W_heads': _L0_gnn_in['W_heads'], 'L0_gnn_a_heads': _L0_gnn_in['a_heads'], 'L0_gnn_W_out': _L0_gnn_in['W_out'], 'L0_gnn_a_out': _L0_gnn_in['a_out'], 'L0_gnn_w1': _L0_gnn_in['w1'], 'L0_gnn_b1': _L0_gnn_in['b1'], 'L0_gnn_w2': _L0_gnn_in['w2'], 'L0_gnn_b2': _L0_gnn_in['b2'], 'L0_gnn_ln_gamma': _L0_gnn_in['ln_gamma'], 'L0_gnn_ln_beta': _L0_gnn_in['ln_beta'], 'L1_gnn_W': _L1_gnn_in['W'], 'L1_gnn_a': _L1_gnn_in['a']}

def reference(x, adj, L0_gnn_W_heads, L0_gnn_a_heads, L0_gnn_W_out, L0_gnn_a_out, L0_gnn_w1, L0_gnn_b1, L0_gnn_w2, L0_gnn_b2, L0_gnn_ln_gamma, L0_gnn_ln_beta, L1_gnn_W, L1_gnn_a):
    import jax
    import jax.numpy as jnp

    def _L0_gnn_ref(enc_inputs, adj, W_heads, a_heads, W_out, a_out, w1, b1, w2, b2, ln_gamma, ln_beta):
        import jax, jax.numpy as jnp
        import numpy as np
        LEAKY_ALPHA = 0.01
        NEG_INF = -1000000000.0
        LN_EPS = 1e-05

        def _gat_heads(x, adj, W, a):
            O = W.shape[-1]
            Wh = jnp.einsum('bnf,hfo->bhno', x, W)
            f1 = jnp.einsum('bhno,ho->bhn', Wh, a[:, :O])
            f2 = jnp.einsum('bhno,ho->bhn', Wh, a[:, O:])
            e = f1[:, :, :, None] + f2[:, :, None, :]
            e = jnp.where(e > 0, e, LEAKY_ALPHA * e)
            e = jnp.where(adj[None, None] > 0, e, NEG_INF)
            attn = jax.nn.softmax(e, axis=-1)
            return jnp.einsum('bhnm,bhmo->bhno', attn, Wh)
        B, N, _ = enc_inputs.shape
        h = jax.nn.elu(_gat_heads(enc_inputs, adj, W_heads, a_heads))
        h = jnp.transpose(h, (0, 2, 1, 3)).reshape(B, N, -1)
        out = _gat_heads(h, adj, W_out[None], a_out[None])[:, 0]
        out = jax.nn.elu(out)
        ffn = jnp.maximum(out @ w1 + b1, 0.0) @ w2 + b2
        y = ffn + out
        mu = jnp.mean(y, axis=-1, keepdims=True)
        var = jnp.var(y, axis=-1, keepdims=True)
        return (y - mu) / jnp.sqrt(var + LN_EPS) * ln_gamma + ln_beta

    def _L1_gnn_ref(X, A, W, a):
        import jax, jax.numpy as jnp
        import numpy as np
        B, N, F, F1 = (512, 75, 256, 128)
        NEG = -1000000000.0
        ALPHA = 0.2
        h = jnp.einsum('bnf,fo->bno', X, W)
        att_self = jnp.einsum('bno,od->bnd', h, a[0])
        att_neigh = jnp.einsum('bno,od->bnd', h, a[1])
        e = att_self + jnp.swapaxes(att_neigh, 1, 2)
        e = jax.nn.leaky_relu(e, ALPHA)
        adj = A.astype(h.dtype)
        e = e + NEG * (1.0 - adj)[None, :, :]
        alpha = jax.nn.softmax(e, axis=-1)
        out = jnp.einsum('bij,bjo->bio', alpha, h)
        return jnp.concatenate([out, h], axis=-1)
    h = jnp.maximum(_layernorm(x, axis=-1), 0.0)
    x = x + _L0_gnn_ref(h, adj, L0_gnn_W_heads, L0_gnn_a_heads, L0_gnn_W_out, L0_gnn_a_out, L0_gnn_w1, L0_gnn_b1, L0_gnn_w2, L0_gnn_b2, L0_gnn_ln_gamma, L0_gnn_ln_beta)
    h = jnp.maximum(_layernorm(x, axis=-1), 0.0)
    x = x + _L1_gnn_ref(h, adj, L1_gnn_W, L1_gnn_a)
    return x

_drawn_inputs = setup_inputs


def setup_inputs(seed=0):
    import zlib

    import numpy as np

    out = dict(_drawn_inputs(seed))
    spreads = {'L0_gnn_b1': (0.0, 0.1),
     'L0_gnn_b2': (0.0, 0.1),
     'L0_gnn_ln_gamma': (1.0, 0.2),
     'L0_gnn_ln_beta': (0.0, 0.1)}
    factors = {}
    for name, (base, spread) in spreads.items():
        noise = np.random.default_rng([zlib.crc32(name.encode()), seed]).standard_normal(out[name].shape)
        drawn = base * np.exp(spread * noise) if base else spread * noise
        out[name] = jnp.asarray(drawn.astype(out[name].dtype))
    for name, factor in factors.items():
        out[name] = (out[name] * factor).astype(out[name].dtype)
    return out
```

```python
from contextlib import ExitStack

import concourse.bass as bass
from concourse import mybir

F32 = mybir.dt.float32
F32R = mybir.dt.float32r
I32 = mybir.dt.int32
ALU = mybir.AluOpType
ACT = mybir.ActivationFunctionType

P = 128
NORM, VALUES, HEADS, MERGE, FFN, LAST = range(6)
STAGES = 6
LN_EPS = 1e-5
BIG = 1e30
NEG = 1e9


class Unit:

    def __init__(self, name, stage, head, slope):
        self.name, self.stage, self.head, self.slope = name, stage, head, slope


def build_gat(nc, x, adj, W_heads, a_heads, W_out, a_out, w1, b1, w2, b2, gamma, beta, W_last, a_last, out):
    NB, N, D = x.shape
    H = W_heads.shape[0]
    O1 = W_last.shape[1]
    M = N // P
    K = D // P
    KH = H * D // P
    F = 2 * H
    CHUNKS = 3
    VW = (F + H * D) // CHUNKS
    assert N == D == 2 * P and H == 4 and O1 == P and W_heads.shape[2] == D

    UNITS = {u.name: u for u in (
        Unit("h0", HEADS, 0, 0.01), Unit("h1", HEADS, 1, 0.01), Unit("h2", HEADS, 2, 0.01),
        Unit("h3", HEADS, 3, 0.01), Unit("merge", MERGE, 0, 0.01), Unit("last", LAST, 0, 0.2))}
    NAMES = list(UNITS)
    ROWS = ("h0", "h1", "h2", "merge", "h3", "last")
    TURNS = ("h0", "h1", "h2", "merge", "h3", "last")
    ATTENDS = ("h0", "h1", "h2", "merge", "h3", "last")
    PRODUCTS = ("up", "wo1", "wo0", "hT", "h1T", "y", "last", "val0", "val2", "val4", "val1", "val3", "val5")
    ELUS = [n for n in NAMES if n != "last"]

    with ExitStack() as ctx:
        def sb(name, shape, dt=F32):
            return ctx.enter_context(nc.sbuf_tensor(name, shape, dt))

        def sem(name):
            return ctx.enter_context(nc.semaphore(name))

        def per_unit(name, names=NAMES):
            return {n: sem(f"{name}_{n}") for n in names}

        ps = ctx.enter_context(nc.psum_tensor("ps", [P, 8, 512], F32))
        bank_row = ps[:, 0, :]
        bank_turn = {n: ps[:, 1 + i % 2, :] for i, n in enumerate(TURNS)}
        bank_att = {n: ps[:, 3 + i % 2, :] for i, n in enumerate(ATTENDS)}
        bank_mm = [ps[:, 5, :], ps[:, 6, :], ps[:, 7, :]]

        Wv = [sb(f"Wv_{s}", [P, K, F + H * D], F32R) for s in ("hi", "lo")]
        Wo = [sb(f"Wo_{s}", [P, KH, D + 2], F32R) for s in ("hi", "lo")]
        Wu = [sb(f"Wu_{s}", [P, K, D], F32R) for s in ("hi", "lo")]
        Wd = [sb(f"Wd_{s}", [P, K, D], F32R) for s in ("hi", "lo")]
        Wl = [sb(f"Wl_{s}", [P, K, O1 + 2], F32R) for s in ("hi", "lo")]
        fold = sb("fold", [P, 2 * H * K + 2 * KH + 2 * K])
        a_rows = sb("a_rows", [P, 2 * H * D + 2 * D + 2 * O1])
        b2_rows = sb("b2_rows", [2, D])
        b2_split = sb("b2_split", [2, D], F32R)
        second = sb("second", [2, 1])
        ones2 = sb("ones2", [2, P], F32R)
        b1_col = sb("b1_col", [P, K])
        gamma_rows = sb("gamma_rows", [P, D])
        beta_rows = sb("beta_rows", [P, 1, D])
        ident = sb("ident", [P, P])
        ident_r = sb("ident_r", [P, P], F32R)
        half_neg = sb("half_neg", [P, M])
        adj_sb = sb("adj_sb", [P, M, N], I32)
        mask_first = sb("mask_first", [P, M, N])
        mask_last = sb("mask_last", [P, M, N])

        x_in = [sb(f"x_in{i}", [P, M, D]) for i in range(2)]
        x_res = [sb(f"x_res{i}", [P, M, D]) for i in range(2)]
        xn = [sb(f"xn{i}", [P, M, D]) for i in range(2)]
        hT = [sb(f"hT_{s}", [P, K, N], F32R) for s in ("hi", "lo")]
        fcol_heads = [sb(f"fcol_heads{i}", [P, M, 2 * H]) for i in range(2)]
        fcol_one = {"merge": sb("fcol_merge", [P, M, 2]), "last": sb("fcol_last", [P, M, 2])}
        val = [[sb(f"val{i}_{s}", [P, M, F + H * D], F32R) for s in ("hi", "lo")] for i in range(2)]
        cat = [sb(f"cat_{s}", [P, KH, N], F32R) for s in ("hi", "lo")]
        val_merge = [sb(f"val_merge_{s}", [P, M, D], F32R) for s in ("hi", "lo")]
        gatT = [[sb(f"gatT{i}_{s}", [P, K, N], F32R) for s in ("hi", "lo")] for i in range(2)]
        ff = sb("ff", [P, K, N])
        ffT = [sb(f"ffT_{s}", [P, K, N], F32R) for s in ("hi", "lo")]
        y_scaled = sb("y_scaled", [P, M, D])
        x1 = [sb(f"x1_{i}", [P, M, D]) for i in range(2)]
        x1n = [sb(f"x1n{i}", [P, M, D]) for i in range(2)]
        h1T = [sb(f"h1T_{s}", [P, K, N], F32R) for s in ("hi", "lo")]
        val_last = [sb(f"val_last_{s}", [P, M, O1], F32R) for s in ("hi", "lo")]
        result = [sb(f"result{i}", [P, M, D]) for i in range(2)]
        LNS = {"x": NORM, "y": FFN, "x1": FFN}
        ln_stats = {n: sb(f"stats_{n}", [P, M, 6]) for n in LNS}
        moments = {n: sb(f"moments_{n}", [P, M, 2]) for n in LNS}
        var_eps = {n: sb(f"var_eps_{n}", [P, M]) for n in LNS}
        mean_neg = {n: sb(f"mean_neg_{n}", [P, M]) for n in LNS}
        rstd = {n: sb(f"rstd_{n}", [P, M]) for n in LNS}

        work = sb("work", [P, len(NAMES) + len(ELUS), M * N])
        probs = {n: work[:, i, :].rearrange("p (m n) -> p m n", m=M) for i, n in enumerate(NAMES)}
        elu = {n: work[:, len(NAMES) + i, :] for i, n in enumerate(ELUS)}
        probsT_two = [[sb(f"probsT{i}_{s}", [P, M, N], F32R) for s in ("hi", "lo")] for i in range(2)]
        probsT = {n: probsT_two[i % 2] for i, n in enumerate(TURNS)}
        row_min = {n: sb(f"row_min_{n}", [P, M]) for n in NAMES}
        row_sum = {n: sb(f"row_sum_{n}", [P, M]) for n in NAMES}
        row_rec = {n: sb(f"row_rec_{n}", [P, M]) for n in NAMES}

        row_made = per_unit("row_made")
        scored = per_unit("scored")
        leaked = per_unit("leaked")
        masked = per_unit("masked")
        exped = per_unit("exped")
        inverted = per_unit("inverted")
        scaled = per_unit("scaled", ELUS)
        turned = per_unit("turned")
        turned_hi = per_unit("turned_hi")
        turned_lo = per_unit("turned_lo")
        attended = per_unit("attended")
        elu_exp = per_unit("elu_exp", ELUS)
        elu_clip = per_unit("elu_clip", ELUS)
        elu_done = per_unit("elu_done", ELUS)
        elu_hi = per_unit("elu_hi", ELUS)
        elu_lo = per_unit("elu_lo", ELUS)
        ln_chain = {n: sem(f"ln_chain_{n}") for n in LNS}
        ln_rstd = {n: sem(f"ln_rstd_{n}") for n in LNS}
        x_loaded = [sem(f"x_loaded{i}") for i in range(2)]
        xn_done = sem("xn_done")
        hT_turned, hT_hi, hT_lo = sem("hT_turned"), sem("hT_hi"), sem("hT_lo")
        fcol_kept = sem("fcol_kept")
        val_made, val_hi, val_lo = sem("val_made"), sem("val_hi"), sem("val_lo")
        wo_made, wo_hi, wo_lo = sem("wo_made"), sem("wo_hi"), sem("wo_lo")
        up_made, up_relu, up_hi, up_lo = sem("up_made"), sem("up_relu"), sem("up_hi"), sem("up_lo")
        y_made, y_scaled_done, x1_done, x1n_done = sem("y_made"), sem("y_scaled_done"), sem("x1_done"), sem("x1n_done")
        res_loaded = [sem(f"res_loaded{i}") for i in range(2)]
        res_beta = sem("res_beta")
        h1T_turned, h1T_hi, h1T_lo = sem("h1T_turned"), sem("h1T_hi"), sem("h1T_lo")
        last_made, last_hi, last_lo = sem("last_made"), sem("last_hi"), sem("last_lo")
        result_left = sem("result_left")
        stored = [sem(f"stored{i}") for i in range(2)]
        wt_loaded = [sem("wt_loaded"), sem("wt_loaded_late")]
        set_up_pool, set_up_dve = sem("set_up_pool"), sem("set_up_dve")
        set_up_done = sem("set_up_done")

        class Step:

            def __init__(self, eng, t=None, pair=None, odd=0, kept=None):
                self.eng, self.t, self.pair, self.odd, self.kept = eng, t, pair, odd, kept

            def runs(self, stage):
                return self.t is None or 0 <= self.t - stage < NB

            def parity(self, stage):
                return (self.odd - stage) % 2 if self.t is None else (self.t - stage) % 2

            def graph(self, stage):
                return 2 * self.pair + (self.odd - stage) if self.t is None else self.t - stage

            def linear(self, slope, offset):
                if (slope, offset) not in self.kept:
                    self.kept[slope, offset] = self.eng.snap(slope * self.pair + offset)
                return self.kept[slope, offset]

            def after(self, semaphore, stage, back=0, per=1, i=None):
                i = per if i is None else i
                if self.t is None:
                    return semaphore, self.linear(2 * per, per * (self.odd - stage - back) + i)
                b = self.t - stage - back
                if b < 0:
                    return set_up_done, 1
                return semaphore, per * b + i if b < NB else per * NB

            def after_dma(self, pair_of, stage, back=0):
                if self.t is None:
                    b = self.odd - stage - back
                    return pair_of[b % 2], self.linear(16, 16 * (b // 2 + 1))
                b = self.t - stage - back
                if b < 0:
                    return set_up_done, 1
                return pair_of[b % 2], 16 * (min(b, NB - 2 + b % 2) // 2 + 1)

            def freed(self, order, use):
                at = [o[0] for o in order].index(use)
                for n in range(1, STAGES * len(order)):
                    back, before = divmod(at - n, len(order))
                    _, stage, semaphore, per, i = order[before]
                    if self.t is None or 0 <= self.t - stage + back < NB:
                        return self.after(semaphore, stage, -back, per, i)
                return set_up_done, 1

        row_order = [(n, UNITS[n].stage, scored[n], 1, 1) for n in ROWS]
        turn_order = {n: [(w, UNITS[w].stage, turned_lo[w], 1, 1) for w in TURNS[i % 2::2]] for i, n in enumerate(TURNS)}
        probsT_order = {n: [(w, UNITS[w].stage, attended[w], 1, 1) for w in TURNS[i % 2::2]] for i, n in enumerate(TURNS)}
        att_order = {n: [(w, UNITS[w].stage, elu_done[w], 1, 1) if w in ELUS else (w, LAST, result_left, 2, 2)
                         for w in ATTENDS[i % 2::2]] for i, n in enumerate(ATTENDS)}
        ATTENDED_LAST = [n for n in ATTENDS if n in ("h0", "h1", "h2", "h3")][-1]
        SCORED_LAST = [n for n in ROWS if n in ("h0", "h1", "h2", "h3")][-1]
        VALS, MERGES = [[int(n[-1]) for n in PRODUCTS if n.startswith(k)] for k in ("val", "wo")]
        freed_by = {
            "h1T": (LAST, h1T_lo, 1, 1), "hT": (VALUES, hT_lo, 1, 1), "last": (LAST, last_lo, 3, 3),
            "up": (FFN, up_relu, 1, 1), "y": (FFN, y_scaled_done, 1, 1),
            **{f"val{q}": (VALUES, val_lo, CHUNKS * M, VALS.index(q) + 1) for q in range(CHUNKS * M)},
            **{f"wo{m}": (MERGE, wo_lo, 4, 2 * MERGES.index(m) + 2) for m in range(M)}}
        mm_uses = [(n, *freed_by[n]) for n in PRODUCTS]
        mm_at = {u[0]: i % 3 for i, u in enumerate(mm_uses)}
        mm_order = [mm_uses[i::3] for i in range(3)]

        def bank(use):
            return bank_mm[mm_at[use]]

        STEPS = NB + STAGES - 1
        FIRST = STAGES + STAGES % 2
        LASTP = NB // 2

        def every_step(eng, body):
            for t in range(FIRST):
                body(Step(eng, t=t))
            with eng.Fori(FIRST // 2, LASTP) as pair:
                kept = {}
                for odd in range(2):
                    body(Step(eng, pair=pair, odd=odd, kept=kept))
            for t in range(2 * LASTP, STEPS):
                body(Step(eng, t=t))

        def fold_heads(k):
            return fold[:, 2 * H * k:2 * H * (k + 1)]
        F_OUT = 2 * H * K
        F_LAST = F_OUT + 2 * KH

        def elu_from(n):
            return elu[n].rearrange("p (k n) -> p k n", k=K)

        def elu_to(s, n):
            if n == "merge":
                return [t[:] for t in gatT[s.parity(MERGE)]]
            return [t[:, K * UNITS[n].head:K * (UNITS[n].head + 1), :] for t in cat]

        def graph_rows(tensor, s, stage):
            return tensor.rearrange("b (p m) f -> b p m f", m=M)[s.graph(stage)]

        block = ctx.enter_context(nc.Block())

        @block.sync
        def _(sp):
            flat = work[:, :, :].rearrange("p a b -> p (a b)")
            for k in range(K):
                sp.dma_start(flat[:, k * H * D:(k + 1) * H * D].rearrange("p (h o) -> p h o", h=H),
                             W_heads.rearrange("h (k p) o -> k p h o", p=P)[k]).then_inc(wt_loaded[0], 16)
            rows = a_rows[:, 0:2 * H * D]
            sp.dma_start(rows, a_heads.rearrange("(a h) d -> a (h d)", a=1).to_broadcast([P, 2 * H * D])).then_inc(wt_loaded[0], 16)
            sp.dma_start(adj_sb[:], adj.rearrange("(p m) n -> p m n", m=M)).then_inc(wt_loaded[0], 16)
            for b in range(2):
                sp.dma_start(x_in[b][:], x.rearrange("b (p m) f -> b p m f", m=M)[b]).then_inc(x_loaded[b], 16)
            o = K * H * D
            sp.dma_start(flat[:, o:o + KH * D].rearrange("p (k o) -> p k o", k=KH),
                         W_out.rearrange("(k p) o -> p k o", p=P)).then_inc(wt_loaded[1], 16)
            o += KH * D
            for w in (w1, w2):
                sp.dma_start(flat[:, o:o + K * D].rearrange("p (k o) -> p k o", k=K),
                             w.rearrange("(k p) o -> p k o", p=P)).then_inc(wt_loaded[1], 16)
                o += K * D
            sp.dma_start(flat[:, o:o + K * O1].rearrange("p (k o) -> p k o", k=K),
                         W_last.rearrange("(k p) o -> p k o", p=P)).then_inc(wt_loaded[1], 16)
            o = 2 * H * D
            sp.dma_start(a_rows[:, o:o + 2 * D], a_out.rearrange("(a d) -> a d", a=1).to_broadcast([P, 2 * D])).then_inc(wt_loaded[1], 16)
            o += 2 * D
            sp.dma_start(a_rows[:, o:o + 2 * O1], a_last.rearrange("s o (a) -> a (s o)", a=1).to_broadcast([P, 2 * O1])).then_inc(wt_loaded[1], 16)
            sp.dma_start(b2_rows[:], b2.rearrange("(a d) -> a d", a=1).to_broadcast([2, D])).then_inc(wt_loaded[1], 16)
            sp.dma_start(gamma_rows[:], gamma.rearrange("(a d) -> a d", a=1).to_broadcast([P, D])).then_inc(wt_loaded[1], 16)
            sp.dma_start(beta_rows[:, 0, :], beta.rearrange("(a d) -> a d", a=1).to_broadcast([P, D])).then_inc(wt_loaded[1], 16)
            with nc.allow_non_contiguous_dma(reason="256 values, once"):
                sp.dma_start(b1_col[:], b1.rearrange("(k p) -> p k", p=P)).then_inc(wt_loaded[1], 16)

            def step(s):
                if s.t is None or 0 <= s.t and s.t + 2 < NB:
                    if s.t is not None or s.odd < 9:
                        load_x(s)
                if s.runs(FFN - 1):
                    sp.wait_ge(*s.after(x1_done, FFN - 1, back=2))
                    par = s.parity(FFN - 1)
                    sp.dma_start(x_res[par][:], graph_rows(x, s, FFN - 1)).then_inc(res_loaded[par], 16)
                if s.runs(LAST):
                    sp.wait_ge(*s.after(result_left, LAST, per=2))
                    par = s.parity(LAST)
                    sp.dma_start(graph_rows(out, s, LAST), result[par][:]).then_inc(stored[par], 16)

            def load_x(s):
                sp.wait_ge(*s.after(xn_done, NORM))
                par = s.parity(NORM)
                sp.dma_start(x_in[par][:], graph_rows(x, s, NORM - 2)).then_inc(x_loaded[par], 16)

            for t in range(FIRST):
                step(Step(sp, t=t))
            with sp.Fori(FIRST // 2, LASTP - 1) as pair:
                kept = {}
                for odd in range(2):
                    step(Step(sp, pair=pair, odd=odd, kept=kept))
            for t in range(2 * LASTP - 2, STEPS):
                step(Step(sp, t=t))
            for par in range(2):
                sp.wait_ge(stored[par], 16 * (NB // 2))

        @block.gpsimd
        def _(pool):
            nc.gpsimd.memset(ident[:], 0.0).then_inc(set_up_pool, 1)
            nc.gpsimd.memset(half_neg[:], -0.5).then_inc(set_up_pool, 1)
            nc.gpsimd.memset(second[:], 1.0).then_inc(set_up_pool, 1)
            pool.wait_ge(set_up_pool, 3)
            nc.gpsimd.affine_select(out=ident[:], in_=ident[:], compare_op=ALU.not_equal, fill=1.0, base=0,
                                    pattern=[[-1, P]], channel_multiplier=1).then_inc(set_up_pool, 1)
            nc.gpsimd.memset(second[0:1, :], 0.0).then_inc(set_up_pool, 1)

            def rsqrt(s, n):
                if not s.runs(LNS[n]):
                    return
                pool.wait_ge(*s.after(ln_chain[n], LNS[n], per=3))
                nc.gpsimd.tensor_tensor(rstd[n][:], var_eps[n][:], half_neg[:], ALU.pow).then_inc(ln_rstd[n], 1)

            def normalise(s, n, src, dst, done):
                pool.wait_ge(*s.after(ln_rstd[n], LNS[n]))
                pool.nop(nofuse=True)
                for m in range(M):
                    last = nc.gpsimd.tensor_scalar(dst[:, m, :], src[:, m, :], mean_neg[n][:, m:m + 1],
                                                   rstd[n][:, m:m + 1], ALU.add, ALU.mult)
                last.then_inc(done, 1)

            def norm_x(s):
                if not s.runs(NORM):
                    return
                pool.wait_ge(*s.after(hT_turned, NORM, back=2))
                normalise(s, "x", x_in[s.parity(NORM)], xn[s.parity(NORM)], xn_done)

            def norm_x1(s):
                if not s.runs(FFN):
                    return
                pool.wait_ge(*s.after(h1T_turned, FFN, back=2))
                normalise(s, "x1", x1[s.parity(FFN)], x1n[s.parity(FFN)], x1n_done)

            def residual(s):
                if not s.runs(FFN):
                    return
                pool.wait_ge(*s.after_dma(res_loaded, FFN))
                par = s.parity(FFN)
                nc.gpsimd.tensor_tensor(x_res[par][:], x_res[par][:], beta_rows[:].to_broadcast([P, M, D]),
                                        ALU.add).then_inc(res_beta, 1)

            def ffn_hi(s):
                if not s.runs(FFN):
                    return
                pool.wait_ge(*s.after(up_relu, FFN))
                pool.wait_ge(*s.after(y_made, FFN, back=1))
                pool.nop(nofuse=True)
                nc.gpsimd.tensor_scalar(ffT[0][:], ff[:], 1.0, 0.0, ALU.mult, ALU.add).then_inc(up_hi, 1)

            def scale(s, n):
                u = UNITS[n]
                if not s.runs(u.stage):
                    return
                pool.wait_ge(*s.after(inverted[n], u.stage))
                pool.nop(nofuse=True)
                for m in range(M):
                    last = nc.gpsimd.tensor_scalar(probs[n][:, m, :], probs[n][:, m, :], row_rec[n][:, m:m + 1],
                                                   1.0, ALU.mult, ALU.mult)
                last.then_inc(scaled[n], 1)

            def split_hi(s, n):
                u = UNITS[n]
                if not s.runs(u.stage):
                    return
                pool.wait_ge(*s.after(elu_done[n], u.stage))
                if n == "merge":
                    pool.wait_ge(*s.after(y_made, MERGE + 2))
                    pool.nop(nofuse=True)
                else:
                    pool.wait_ge(*s.after(wo_made, HEADS, back=1, per=2))
                    pool.nop(nofuse=True)
                nc.gpsimd.tensor_scalar(elu_to(s, n)[0], elu_from(n), 1.0, 0.0, ALU.mult, ALU.add).then_inc(elu_hi[n], 1)

            def split_lo(s, n):
                u = UNITS[n]
                if not s.runs(u.stage):
                    return
                hi, lo = elu_to(s, n)
                pool.wait_ge(*s.after(elu_hi[n], u.stage))
                nc.gpsimd.tensor_tensor(lo, elu_from(n), hi.bitcast(F32), ALU.subtract).then_inc(elu_lo[n], 1)

            def step(s):
                residual(s)
                scale(s, "h0")
                ffn_hi(s)
                scale(s, "h1")
                scale(s, "h2")
                rsqrt(s, "x")
                split_hi(s, "h0")
                scale(s, "merge")
                split_lo(s, "h0")
                rsqrt(s, "y")
                scale(s, "h3")
                split_hi(s, "h1")
                split_hi(s, "h2")
                split_lo(s, "h2")
                split_lo(s, "h1")
                split_hi(s, "merge")
                split_lo(s, "merge")
                split_hi(s, "h3")
                split_lo(s, "h3")
                rsqrt(s, "x1")
                norm_x(s)
                norm_x1(s)

            pool.wait_ge(set_up_done, 1)
            every_step(pool, step)

        @block.scalar
        def _(act):
            def hi_copy(dst, src, done, func=ACT.Identity):
                nc.scalar.activation(dst, src, func).then_inc(done, 1)

            def scores(s, n):
                u = UNITS[n]
                if not s.runs(u.stage):
                    return
                act.wait_ge(*s.after(row_made[n], u.stage))
                act.wait_ge(*s.after(turned[n], u.stage, back=1))
                col = fcol_heads[s.parity(HEADS)] if u.stage == HEADS else fcol_one[n]
                for m in range(M):
                    last = nc.scalar.activation(probs[n][:, m, :], bank_row[:, 0:N], ACT.Identity,
                                                bias=col[:, m, u.head:u.head + 1])
                last.then_inc(scored[n], 1)

            def exps(s, n):
                u = UNITS[n]
                if not s.runs(u.stage):
                    return
                act.wait_ge(*s.after(masked[n], u.stage))
                for m in range(M):
                    last = nc.scalar.activation(probs[n][:, m, :], probs[n][:, m, :], ACT.Exp, scale=-1.0,
                                                bias=row_min[n][:, m:m + 1], accum_out=row_sum[n][:, m:m + 1])
                last.then_inc(exped[n], 1)

            def turn_hi(s, n):
                u = UNITS[n]
                if not s.runs(u.stage):
                    return
                act.wait_ge(*s.after(turned[n], u.stage))
                act.wait_ge(*s.freed(probsT_order[n], n))
                hi_copy(probsT[n][0][:].rearrange("p m n -> p (m n)"), bank_turn[n], turned_hi[n])

            def elu_exps(s, n):
                u = UNITS[n]
                if not s.runs(u.stage):
                    return
                act.wait_ge(*s.after(attended[n], u.stage))
                act.wait_ge(*s.after(elu_lo[n], u.stage, back=1))
                nc.scalar.activation(elu[n], bank_att[n], ACT.Exp).then_inc(elu_exp[n], 1)

            def clip(s, n):
                u = UNITS[n]
                if not s.runs(u.stage):
                    return
                act.wait_ge(*s.after(elu_exp[n], u.stage))
                nc.scalar.activation(elu[n], elu[n], ACT.Relu, bias=1.0, scale=-1.0).then_inc(elu_clip[n], 1)

            def turn_x(s):
                if not s.runs(VALUES):
                    return
                act.wait_ge(*s.after(hT_turned, VALUES))
                act.wait_ge(*s.after(val_made, VALUES, back=1, per=CHUNKS * M))
                hi_copy(hT[0][:].rearrange("p k n -> p (k n)"), bank("hT"), hT_hi, ACT.Relu)

            def value_hi(s, q):
                if not s.runs(VALUES):
                    return
                m, c = divmod(q, CHUNKS)
                act.wait_ge(*s.after(val_made, VALUES, per=CHUNKS * M, i=VALS.index(q) + 1))
                act.wait_ge(*s.after(attended[ATTENDED_LAST], HEADS + 1))
                hi_copy(val[s.parity(VALUES)][0][:, m, c * VW:(c + 1) * VW], bank(f"val{q}")[:, 0:VW], val_hi)

            def merge_hi(s, m):
                if not s.runs(MERGE):
                    return
                act.wait_ge(*s.after(wo_made, MERGE, per=2, i=MERGES.index(m) + 1))
                act.wait_ge(*s.after(attended["merge"], MERGE, back=1))
                hi_copy(val_merge[0][:, m, :], bank(f"wo{m}")[:, 0:D], wo_hi)

            def ffn_relu(s):
                if not s.runs(FFN):
                    return
                act.wait_ge(*s.after(up_made, FFN))
                act.wait_ge(*s.after(up_lo, FFN, back=1))
                for k in range(K):
                    last = nc.scalar.activation(ff[:, k, :], bank("up")[:, k * N:(k + 1) * N], ACT.Relu,
                                                bias=b1_col[:, k:k + 1])
                last.then_inc(up_relu, 1)

            def turn_x1(s):
                if not s.runs(LAST):
                    return
                act.wait_ge(*s.after(h1T_turned, LAST))
                act.wait_ge(*s.after(last_made, LAST, back=1))
                hi_copy(h1T[0][:].rearrange("p k n -> p (k n)"), bank("h1T"), h1T_hi, ACT.Relu)

            def last_hi_copy(s):
                if not s.runs(LAST):
                    return
                act.wait_ge(*s.after(last_made, LAST))
                act.wait_ge(*s.after(attended["last"], LAST, back=1))
                hi_copy(val_last[0][:], bank("last").rearrange("p (m o) -> p m o", m=M)[:, :, 0:O1], last_hi)

            def step(s):
                scores(s, "h0")
                ffn_relu(s)
                scores(s, "h1")
                exps(s, "h0")
                scores(s, "h2")
                merge_hi(s, 1)
                exps(s, "h1")
                merge_hi(s, 0)
                turn_hi(s, "h0")
                turn_x(s)
                turn_x1(s)
                turn_hi(s, "h1")
                scores(s, "merge")
                exps(s, "h2")
                elu_exps(s, "h0")
                clip(s, "h0")
                scores(s, "h3")
                exps(s, "merge")
                last_hi_copy(s)
                turn_hi(s, "h2")
                value_hi(s, 0)
                exps(s, "h3")
                elu_exps(s, "h1")
                scores(s, "last")
                clip(s, "h1")
                turn_hi(s, "merge")
                elu_exps(s, "h2")
                value_hi(s, 2)
                clip(s, "h2")
                turn_hi(s, "h3")
                value_hi(s, 4)
                exps(s, "last")
                value_hi(s, 1)
                elu_exps(s, "merge")
                turn_hi(s, "last")
                clip(s, "merge")
                elu_exps(s, "h3")
                clip(s, "h3")
                value_hi(s, 3)
                value_hi(s, 5)

            act.wait_ge(set_up_done, 1)
            every_step(act, step)

        @block.vector
        def _(dve):
            done = [0]

            def chained(instruction):
                done[0] += 1
                instruction.then_inc(set_up_dve, 1)

            def settle():
                dve.wait_ge(set_up_dve, done[0])

            dve.wait_ge(wt_loaded[0], 16 * (K + 2))
            keys = adj_sb[:].rearrange("p m (q w) -> p m w q", w=M)
            for m in range(M):
                chained(nc.vector.tensor_scalar(mask_first[:, m, :].rearrange("p (w q) -> p w q", w=M), keys[:, m],
                                                0.0, BIG, ALU.is_le, ALU.mult))
                chained(nc.vector.tensor_scalar(mask_last[:, m, :].rearrange("p (w q) -> p w q", w=M), keys[:, m],
                                                -NEG, NEG, ALU.mult, ALU.add))
            flat = work[:, :, :].rearrange("p a b -> p (a b)")
            scratch = y_scaled[:].rearrange("p m d -> p (m d)")

            def fold_vector(w, a, dst, width):
                settle()
                chained(nc.vector.tensor_tensor_reduce(scratch[:, 0:width], w, a, -1.0, 0.0, ALU.mult, ALU.add, dst))

            for k in range(K):
                for h in range(H):
                    for side in range(2):
                        fold_vector(flat[:, (k * H + h) * D:(k * H + h + 1) * D],
                                    a_rows[:, (2 * h + side) * D:(2 * h + side + 1) * D],
                                    fold_heads(k)[:, side * H + h:side * H + h + 1], D)

            def split_to(pair, src, width=None):
                hi, lo = pair
                chained(nc.vector.tensor_copy(hi, src))
                settle()
                chained(nc.vector.tensor_tensor(lo, src, hi.bitcast(F32), ALU.subtract))

            for k in range(K):
                split_to([w[:, k, F:] for w in Wv], flat[:, k * H * D:(k + 1) * H * D])
                settle()
                split_to([w[:, k, 0:F] for w in Wv], fold_heads(k))
            dve.wait_ge(wt_loaded[1], 16 * 10)
            dve.wait_ge(set_up_pool, 5)
            o = K * H * D
            a = 2 * H * D
            for k in range(KH):
                for side in range(2):
                    fold_vector(flat[:, o + k * D:o + (k + 1) * D], a_rows[:, a + side * D:a + (side + 1) * D],
                                fold[:, F_OUT + 2 * k + side:F_OUT + 2 * k + side + 1], D)
            settle()
            split_to([w[:, :, 0:D] for w in Wo], flat[:, o:o + KH * D].rearrange("p (k o) -> p k o", k=KH))
            split_to([w[:, :, D:D + 2] for w in Wo], fold[:, F_OUT:F_OUT + 2 * KH].rearrange("p (k s) -> p k s", s=2))
            o += KH * D
            a += 2 * D
            for pair in (Wu, Wd):
                split_to([w[:] for w in pair], flat[:, o:o + K * D].rearrange("p (k o) -> p k o", k=K))
                o += K * D
            for k in range(K):
                for side in range(2):
                    fold_vector(flat[:, o + k * O1:o + (k + 1) * O1], a_rows[:, a + side * O1:a + (side + 1) * O1],
                                fold[:, F_LAST + 2 * k + side:F_LAST + 2 * k + side + 1], O1)
            settle()
            split_to([w[:, :, 0:O1] for w in Wl], flat[:, o:o + K * O1].rearrange("p (k o) -> p k o", k=K))
            split_to([w[:, :, O1:O1 + 2] for w in Wl], fold[:, F_LAST:F_LAST + 2 * K].rearrange("p (k s) -> p k s", s=2))
            chained(nc.vector.tensor_copy(b2_split[:], b2_rows[:]))
            chained(nc.vector.tensor_scalar(second[:], second[:], -1.0, None, ALU.mult))
            settle()
            chained(nc.vector.scalar_tensor_tensor(out=b2_split[:], in0=b2_split[:].bitcast(F32), scalar=second[:, 0:1],
                                                   in1=b2_rows[:], op0=ALU.mult, op1=ALU.add))
            chained(nc.vector.tensor_copy(ident_r[:], ident[:]))
            chained(nc.vector.tensor_scalar(ones2[:], ident[0:2, :], 0.0, 1.0, ALU.mult, ALU.add))
            settle()
            nc.vector.memset(scratch[:, 0:1], 0.0).then_inc(set_up_done, 1)
            dve.wait_ge(set_up_done, 1)

            def stats(s, n, src):
                dve.wait_ge(*s.after(ln_rstd[n], LNS[n], back=1))
                dve.wait_ge(*s.after({"x": xn_done, "y": x1_done, "x1": x1n_done}[n], LNS[n], back=1))
                for m in range(M):
                    last = nc.vector.bn_stats(ln_stats[n][:, m, :], src(m))
                last.then_inc(ln_chain[n], 1)

            def aggregate(s, n):
                if not s.runs(LNS[n]):
                    return
                dve.wait_ge(*s.after(ln_chain[n], LNS[n], per=3, i=1))
                dve.nop(nofuse=True)
                for m in range(M):
                    last = nc.vector.bn_aggr(moments[n][:, m, :], ln_stats[n][:, m, :])
                last.then_inc(ln_chain[n], 1)

            def mean_and_var(s, n):
                if not s.runs(LNS[n]):
                    return
                dve.wait_ge(*s.after(ln_chain[n], LNS[n], per=3, i=2))
                nc.vector.tensor_scalar(mean_neg[n][:], moments[n][:, :, 0], -1.0, None, ALU.mult)
                nc.vector.tensor_scalar(var_eps[n][:], moments[n][:, :, 1], LN_EPS, None, ALU.add).then_inc(ln_chain[n], 1)

            def stats_x(s):
                if s.runs(NORM):
                    dve.wait_ge(*s.after_dma(x_loaded, NORM))
                    stats(s, "x", lambda m: x_in[s.parity(NORM)][:, m, :])

            def stats_y(s):
                if s.runs(FFN):
                    dve.wait_ge(*s.after(y_made, FFN))
                    stats(s, "y", lambda m: bank("y")[:, m * D:(m + 1) * D])

            def stats_x1(s):
                if s.runs(FFN):
                    dve.wait_ge(*s.after(x1_done, FFN))
                    stats(s, "x1", lambda m: x1[s.parity(FFN)][:, m, :])

            def leak(s, n):
                u = UNITS[n]
                if not s.runs(u.stage):
                    return
                dve.wait_ge(*s.after(scored[n], u.stage))
                nc.vector.scalar_tensor_tensor(out=probs[n], in0=probs[n], scalar=u.slope, in1=probs[n],
                                               op0=ALU.mult, op1=ALU.min).then_inc(leaked[n], 1)

            def mask_and_min(s, n):
                u = UNITS[n]
                if not s.runs(u.stage):
                    return
                dve.wait_ge(*s.after(leaked[n], u.stage))
                dve.nop(nofuse=True)
                mask = mask_last if n == "last" else mask_first
                for m in range(M):
                    last = nc.vector.tensor_tensor_reduce(probs[n][:, m, :], probs[n][:, m, :], mask[:, m, :],
                                                          1.0, 3e38, ALU.add, ALU.min, row_min[n][:, m:m + 1])
                last.then_inc(masked[n], 1)

            def invert(s, n):
                u = UNITS[n]
                if not s.runs(u.stage):
                    return
                dve.wait_ge(*s.after(exped[n], u.stage))
                nc.vector.reciprocal(row_rec[n][:], row_sum[n][:]).then_inc(inverted[n], 1)

            def turn_lo(s, n):
                u = UNITS[n]
                if not s.runs(u.stage):
                    return
                hi, lo = (t[:].rearrange("p m n -> p (m n)") for t in probsT[n])
                dve.wait_ge(*s.after(turned_hi[n], u.stage))
                nc.vector.tensor_tensor(lo, bank_turn[n], hi.bitcast(F32), ALU.subtract).then_inc(turned_lo[n], 1)

            def elus(s, n):
                u = UNITS[n]
                if not s.runs(u.stage):
                    return
                dve.wait_ge(*s.after(elu_clip[n], u.stage))
                nc.vector.scalar_tensor_tensor(out=elu[n], in0=elu[n], scalar=-1.0, in1=bank_att[n],
                                               op0=ALU.mult, op1=ALU.max).then_inc(elu_done[n], 1)

            def relu_lo(pair, src, finished):
                hi, lo = (t[:].rearrange("p k n -> p (k n)") for t in pair)
                nc.vector.scalar_tensor_tensor(out=lo, in0=src, scalar=0.0, in1=hi.bitcast(F32),
                                               op0=ALU.max, op1=ALU.subtract).then_inc(finished, 1)

            def turn_x(s):
                if s.runs(VALUES):
                    dve.wait_ge(*s.after(hT_hi, VALUES))
                    relu_lo(hT, bank("hT"), hT_lo)

            def value_lo(s, q):
                if not s.runs(VALUES):
                    return
                m, c = divmod(q, CHUNKS)
                hi, lo = (t[:, m, c * VW:(c + 1) * VW] for t in val[s.parity(VALUES)])
                dve.wait_ge(*s.after(val_hi, VALUES, per=CHUNKS * M, i=VALS.index(q) + 1))
                if c == 0:
                    dve.wait_ge(*s.after(scored[SCORED_LAST], HEADS + 1))
                    nc.vector.tensor_copy(fcol_heads[s.parity(VALUES)][:, m, :], bank(f"val{q}")[:, 0:F]).then_inc(fcol_kept, 1)
                nc.vector.tensor_tensor(lo, bank(f"val{q}")[:, 0:VW], hi.bitcast(F32), ALU.subtract).then_inc(val_lo, 1)

            def merge_lo(s, m):
                if not s.runs(MERGE):
                    return
                hi, lo = (t[:, m, :] for t in val_merge)
                dve.wait_ge(*s.after(wo_hi, MERGE, per=2, i=MERGES.index(m) + 1))
                nc.vector.tensor_tensor(lo, bank(f"wo{m}")[:, 0:D], hi.bitcast(F32), ALU.subtract).then_inc(wo_lo, 1)
                dve.wait_ge(*s.after(scored["merge"], MERGE, back=1))
                nc.vector.tensor_copy(fcol_one["merge"][:, m, :], bank(f"wo{m}")[:, D:D + 2]).then_inc(wo_lo, 1)

            def ffn_lo(s):
                if not s.runs(FFN):
                    return
                dve.wait_ge(*s.after(up_hi, FFN))
                nc.vector.tensor_tensor(ffT[1][:], ff[:], ffT[0][:].bitcast(F32), ALU.subtract).then_inc(up_lo, 1)

            def scale_y(s):
                if not s.runs(FFN):
                    return
                dve.wait_ge(*s.after(ln_chain["y"], FFN, per=3, i=2))
                for m in range(M):
                    last = nc.vector.scalar_tensor_tensor(out=y_scaled[:, m, :], in0=bank("y")[:, m * D:(m + 1) * D],
                                                          scalar=moments["y"][:, m, 0:1], in1=gamma_rows[:],
                                                          op0=ALU.subtract, op1=ALU.mult)
                last.then_inc(y_scaled_done, 1)

            def make_x1(s):
                if not s.runs(FFN):
                    return
                par = s.parity(FFN)
                dve.wait_ge(*s.after(y_scaled_done, FFN))
                dve.wait_ge(*s.after(ln_rstd["y"], FFN))
                dve.wait_ge(*s.after(res_beta, FFN))
                dve.wait_ge(*s.after(result_left, FFN, back=2, per=2))
                for m in range(M):
                    last = nc.vector.scalar_tensor_tensor(out=x1[par][:, m, :], in0=y_scaled[:, m, :],
                                                          scalar=rstd["y"][:, m:m + 1], in1=x_res[par][:, m, :],
                                                          op0=ALU.mult, op1=ALU.add)
                last.then_inc(x1_done, 1)

            def turn_x1(s):
                if s.runs(LAST):
                    dve.wait_ge(*s.after(h1T_hi, LAST))
                    relu_lo(h1T, bank("h1T"), h1T_lo)

            def last_parts(s):
                if not s.runs(LAST):
                    return
                par = s.parity(LAST)
                hp = bank("last").rearrange("p (m o) -> p m o", m=M)
                dve.wait_ge(*s.after(last_hi, LAST))
                nc.vector.tensor_tensor(val_last[1][:], hp[:, :, 0:O1], val_last[0][:].bitcast(F32),
                                        ALU.subtract).then_inc(last_lo, 1)
                dve.wait_ge(*s.after(scored["last"], LAST, back=1))
                nc.vector.tensor_copy(fcol_one["last"][:], hp[:, :, O1:O1 + 2]).then_inc(last_lo, 1)
                dve.wait_ge(*s.after_dma(stored, LAST, back=2))
                nc.vector.tensor_tensor(result[par][:, :, O1:D], hp[:, :, 0:O1], x1[par][:, :, O1:D],
                                        ALU.add).then_inc(last_lo, 1)

            def last_result(s):
                if not s.runs(LAST):
                    return
                par = s.parity(LAST)
                dve.wait_ge(*s.after(attended["last"], LAST))
                for m in range(M):
                    nc.vector.scalar_tensor_tensor(out=result[par][:, m, 0:O1],
                                                   in0=bank_att["last"][:, m * O1:(m + 1) * O1],
                                                   scalar=row_rec["last"][:, m:m + 1], in1=x1[par][:, m, 0:O1],
                                                   op0=ALU.mult, op1=ALU.add).then_inc(result_left, 1)

            def step(s):
                leak(s, "h0")
                mask_and_min(s, "h0")
                stats_x(s)
                leak(s, "h1")
                mask_and_min(s, "h1")
                aggregate(s, "x")
                invert(s, "h0")
                leak(s, "h2")
                merge_lo(s, 1)
                invert(s, "h1")
                mask_and_min(s, "h2")
                merge_lo(s, 0)
                turn_lo(s, "h0")
                ffn_lo(s)
                turn_x(s)
                turn_lo(s, "h1")
                mean_and_var(s, "x")
                leak(s, "merge")
                turn_x1(s)
                mask_and_min(s, "merge")
                invert(s, "h2")
                elus(s, "h0")
                stats_y(s)
                leak(s, "h3")
                aggregate(s, "y")
                mask_and_min(s, "h3")
                invert(s, "merge")
                last_parts(s)
                turn_lo(s, "h2")
                scale_y(s)
                mean_and_var(s, "y")
                invert(s, "h3")
                leak(s, "last")
                elus(s, "h1")
                value_lo(s, 0)
                mask_and_min(s, "last")
                turn_lo(s, "merge")
                elus(s, "h2")
                turn_lo(s, "h3")
                make_x1(s)
                value_lo(s, 2)
                stats_x1(s)
                invert(s, "last")
                value_lo(s, 4)
                elus(s, "merge")
                value_lo(s, 1)
                turn_lo(s, "last")
                elus(s, "h3")
                value_lo(s, 3)
                value_lo(s, 5)
                aggregate(s, "x1")
                last_result(s)
                mean_and_var(s, "x1")

            every_step(dve, step)

        @block.tensor
        def _(pe):
            def three(out_ap, lhs, rhs, first, final):
                passes = ((lhs[0], rhs[1]), (lhs[1], rhs[0]), (lhs[0], rhs[0]))
                for i, (l, r) in enumerate(passes):
                    ins = nc.tensor.matmul(out_ap, l, r, start=first and i == 0, stop=final and i == 2)
                return ins

            def row(s, n):
                u = UNITS[n]
                if not s.runs(u.stage):
                    return
                if u.stage == HEADS:
                    pe.wait_ge(*s.after(fcol_kept, HEADS, per=M))
                    col, at = fcol_heads[s.parity(HEADS)], H + u.head
                else:
                    pe.wait_ge(*s.after(wo_lo if n == "merge" else last_lo, u.stage, per=4 if n == "merge" else 3, i=None if n == "merge" else 2))
                    col, at = fcol_one[n], 1
                pe.wait_ge(*s.freed(row_order, n))
                for m in range(M):
                    last = nc.tensor.transpose(bank_row[:, m * P:(m + 1) * P],
                                               col[:, m, at:at + 1].to_broadcast([P, P]), ident[:])
                last.then_inc(row_made[n], 1)

            def turn(s, n):
                u = UNITS[n]
                if not s.runs(u.stage):
                    return
                if n == "last":
                    pe.wait_ge(*s.after(exped[n], u.stage))
                else:
                    pe.wait_ge(*s.after(scaled[n], u.stage))
                pe.wait_ge(*s.freed(turn_order[n], n))
                for m in range(M):
                    for j in range(M):
                        last = nc.tensor.transpose(bank_turn[n][:, j * N + m * P:j * N + (m + 1) * P],
                                                   probs[n][:, m, j * P:(j + 1) * P], ident[:])
                last.then_inc(turned[n], 1)

            def attend(s, n):
                u = UNITS[n]
                if not s.runs(u.stage):
                    return
                pe.wait_ge(*s.after(turned_lo[n], u.stage))
                if u.stage == HEADS:
                    pe.wait_ge(*s.after(val_lo, HEADS, per=CHUNKS * M))
                pe.wait_ge(*s.freed(att_order[n], n))
                to = bank_att[n]
                pT = probsT[n]
                if n == "last":
                    for m in range(M):
                        for j in range(M):
                            last = three(to[:, m * O1:(m + 1) * O1], [t[:, j, m * P:(m + 1) * P] for t in pT],
                                         [t[:, j, :] for t in val_last], j == 0, j == M - 1)
                else:
                    v = val[s.parity(HEADS)] if u.stage == HEADS else val_merge
                    for k in range(K):
                        c = (F if u.stage == HEADS else 0) + u.head * D + k * P
                        for j in range(M):
                            last = three(to[:, k * N:(k + 1) * N], [t[:, j, c:c + P] for t in v],
                                         [t[:, j, :] for t in pT], j == 0, j == M - 1)
                last.then_inc(attended[n], 1)

            def turn_nodes(use, src, finished):
                for k in range(K):
                    for m in range(M):
                        last = nc.tensor.transpose(bank(use)[:, k * N + m * P:k * N + (m + 1) * P],
                                                   src[:, m, k * P:(k + 1) * P], ident[:])
                last.then_inc(finished, 1)

            def turn_x(s):
                if not s.runs(VALUES):
                    return
                pe.wait_ge(*s.after(xn_done, VALUES))
                pe.wait_ge(*s.freed(mm_order[mm_at["hT"]], "hT"))
                turn_nodes("hT", xn[s.parity(VALUES)], hT_turned)

            def values(s, q):
                if not s.runs(VALUES):
                    return
                m, c = divmod(q, CHUNKS)
                pe.wait_ge(*s.after(hT_lo, VALUES))
                pe.wait_ge(*s.freed(mm_order[mm_at[f"val{q}"]], f"val{q}"))
                for k in range(K):
                    last = three(bank(f"val{q}")[:, 0:VW], [t[:, k, m * P:(m + 1) * P] for t in hT],
                                 [w[:, k, c * VW:(c + 1) * VW] for w in Wv], k == 0, k == K - 1)
                last.then_inc(val_made, 1)

            def merge(s, m):
                if not s.runs(MERGE):
                    return
                for n in ("h0", "h1", "h2", "h3"):
                    pe.wait_ge(*s.after(elu_lo[n], MERGE))
                pe.wait_ge(*s.freed(mm_order[mm_at[f"wo{m}"]], f"wo{m}"))
                for c in range(KH):
                    last = three(bank(f"wo{m}")[:, 0:D + 2], [t[:, c, m * P:(m + 1) * P] for t in cat],
                                 [w[:, c, :] for w in Wo], c == 0, c == KH - 1)
                last.then_inc(wo_made, 1)

            def ffn_up(s):
                if not s.runs(FFN):
                    return
                g = gatT[s.parity(FFN)]
                pe.wait_ge(*s.after(elu_lo["merge"], FFN))
                pe.wait_ge(*s.freed(mm_order[mm_at["up"]], "up"))
                for d in range(K):
                    for k in range(K):
                        last = three(bank("up")[:, d * N:(d + 1) * N], [w[:, k, d * P:(d + 1) * P] for w in Wu],
                                     [t[:, k, :] for t in g], k == 0, k == K - 1)
                last.then_inc(up_made, 1)

            def ffn_down(s):
                if not s.runs(FFN):
                    return
                g = gatT[s.parity(FFN)]
                pe.wait_ge(*s.after(up_lo, FFN))
                pe.wait_ge(*s.freed(mm_order[mm_at["y"]], "y"))
                for m in range(M):
                    nodes = slice(m * P, (m + 1) * P)
                    to = bank("y")[:, m * D:(m + 1) * D]
                    nc.tensor.matmul(to, ones2[:], b2_split[:], start=True, stop=False)
                    for k in range(K):
                        three(to, [t[:, k, nodes] for t in ffT], [w[:, k, :] for w in Wd], False, False)
                    for k in range(K):
                        for half in (1, 0):
                            last = nc.tensor.matmul(to[:, k * P:(k + 1) * P], g[half][:, k, nodes], ident_r[:],
                                                    start=False, stop=k == K - 1 and half == 0)
                last.then_inc(y_made, 1)

            def turn_x1(s):
                if not s.runs(LAST):
                    return
                pe.wait_ge(*s.after(x1n_done, LAST))
                pe.wait_ge(*s.freed(mm_order[mm_at["h1T"]], "h1T"))
                turn_nodes("h1T", x1n[s.parity(LAST)], h1T_turned)

            def last_values(s):
                if not s.runs(LAST):
                    return
                pe.wait_ge(*s.after(h1T_lo, LAST))
                pe.wait_ge(*s.freed(mm_order[mm_at["last"]], "last"))
                for m in range(M):
                    for k in range(K):
                        last = three(bank("last")[:, m * 256:m * 256 + O1 + 2], [t[:, k, m * P:(m + 1) * P] for t in h1T],
                                     [w[:, k, :] for w in Wl], k == 0, k == K - 1)
                last.then_inc(last_made, 1)

            def step(s):
                row(s, "h0")
                ffn_up(s)
                row(s, "h1")
                merge(s, 1)
                row(s, "h2")
                merge(s, 0)
                turn(s, "h0")
                turn_x(s)
                turn_x1(s)
                row(s, "merge")
                turn(s, "h1")
                attend(s, "h0")
                ffn_down(s)
                row(s, "h3")
                last_values(s)
                turn(s, "h2")
                values(s, 0)
                attend(s, "h1")
                row(s, "last")
                turn(s, "merge")
                attend(s, "h2")
                values(s, 2)
                values(s, 4)
                turn(s, "h3")
                values(s, 1)
                attend(s, "merge")
                turn(s, "last")
                attend(s, "h3")
                values(s, 3)
                values(s, 5)
                attend(s, "last")

            pe.wait_ge(set_up_done, 1)
            every_step(pe, step)


_INS = ["x", "adj", "L0_gnn_W_heads", "L0_gnn_a_heads", "L0_gnn_W_out", "L0_gnn_a_out", "L0_gnn_w1", "L0_gnn_b1",
        "L0_gnn_w2", "L0_gnn_b2", "L0_gnn_ln_gamma", "L0_gnn_ln_beta", "L1_gnn_W", "L1_gnn_a"]


def kernel(**inputs):
    import numpy as np
    import concourse.bacc as bacc
    from concourse import mybir as mb
    from concourse.bass_utils import run_bass_kernel_spmd

    nc = bacc.Bacc("TRN2", target_bir_lowering=False, num_devices=1)
    arrays, args = {}, []
    for name in _INS:
        a = np.ascontiguousarray(inputs[name])
        arrays[f"in_{name}"] = a
        args.append(nc.dram_tensor(f"in_{name}", a.shape, mb.dt.from_np(a.dtype), kind="ExternalInput").ap())
    shape = arrays["in_x"].shape
    args.append(nc.dram_tensor("out_0", shape, mb.dt.float32, kind="ExternalOutput").ap())
    build_gat(nc, *args)
    r = run_bass_kernel_spmd(nc, [arrays], core_ids=[0])
    return r.results[0]["out_0"]
```

```python
from contextlib import ExitStack

import concourse.bass as bass
from concourse import mybir

F32 = mybir.dt.float32
F32R = mybir.dt.float32r
I32 = mybir.dt.int32
ALU = mybir.AluOpType
ACT = mybir.ActivationFunctionType

P = 128
NORM, VALUES, HEADS, MERGE, FFN, LAST = range(6)
STAGES = 6
CONSTANTS = 5
LN_EPS = 1e-5
BIG = 1e30
NEG = 1e9


class Unit:

    def __init__(self, name, stage, head, slope):
        self.name, self.stage, self.head, self.slope = name, stage, head, slope


def build_gat(nc, x, adj, W_heads, a_heads, W_out, a_out, w1, b1, w2, b2, gamma, beta, W_last, a_last, out):
    NB, N, D = x.shape
    H = W_heads.shape[0]
    O1 = W_last.shape[1]
    M = N // P
    K = D // P
    KH = H * D // P
    F = 2 * H
    CHUNKS = 3
    VW = (F + H * D) // CHUNKS
    assert N == D == 2 * P and H == 4 and O1 == P and W_heads.shape[2] == D

    UNITS = {u.name: u for u in (
        Unit("h0", HEADS, 0, 0.01), Unit("h1", HEADS, 1, 0.01), Unit("h2", HEADS, 2, 0.01),
        Unit("h3", HEADS, 3, 0.01), Unit("merge", MERGE, 0, 0.01), Unit("last", LAST, 0, 0.2))}
    NAMES = list(UNITS)
    ROWS = ("h0", "h1", "h2", "merge", "h3", "last")
    TURNS = ("h0", "h1", "h2", "merge", "h3", "last")
    ATTENDS = ("h0", "h1", "h2", "merge", "h3", "last")
    PRODUCTS = ("up", "wo1", "wo0", "hT", "h1T", "y", "last", "val0", "val2", "val4", "val1", "val3", "val5")
    ELUS = [n for n in NAMES if n != "last"]

    with ExitStack() as ctx:
        def sb(name, shape, dt=F32):
            return ctx.enter_context(nc.sbuf_tensor(name, shape, dt))

        def sem(name):
            return ctx.enter_context(nc.semaphore(name))

        def per_unit(name, names=NAMES):
            return {n: sem(f"{name}_{n}") for n in names}

        ps = ctx.enter_context(nc.psum_tensor("ps", [P, 8, 512], F32))
        bank_row = ps[:, 0, :]
        bank_turn = {n: ps[:, 1 + i % 2, :] for i, n in enumerate(TURNS)}
        bank_att = {n: ps[:, 3 + i % 2, :] for i, n in enumerate(ATTENDS)}
        bank_mm = [ps[:, 5, :], ps[:, 6, :], ps[:, 7, :]]

        Wv = [sb(f"Wv_{s}", [P, K, F + H * D], F32R) for s in ("hi", "lo")]
        Wo = [sb(f"Wo_{s}", [P, KH, D + 2], F32R) for s in ("hi", "lo")]
        Wu = [sb(f"Wu_{s}", [P, K, D], F32R) for s in ("hi", "lo")]
        Wd = [sb(f"Wd_{s}", [P, K, D], F32R) for s in ("hi", "lo")]
        Wl = [sb(f"Wl_{s}", [P, K, O1 + 2], F32R) for s in ("hi", "lo")]
        fold = sb("fold", [P, 2 * H * K + 2 * KH + 2 * K])
        a_rows = sb("a_rows", [P, 2 * H * D + 2 * D + 2 * O1])
        b2_rows = sb("b2_rows", [2, D])
        b2_split = sb("b2_split", [2, D], F32R)
        b2_keep = sb("b2_keep", [2, 1])
        ones2 = sb("ones2", [2, P], F32R)
        b1_col = sb("b1_col", [P, K])
        gamma_rows = sb("gamma_rows", [P, D])
        beta_rows = sb("beta_rows", [P, 1, D])
        ident = sb("ident", [P, P])
        half_neg = sb("half_neg", [P, M])
        adj_sb = sb("adj_sb", [P, M, N], I32)
        mask_first = sb("mask_first", [P, M, N])
        mask_last = sb("mask_last", [P, M, N])

        x_in = [sb(f"x_in{i}", [P, M, D]) for i in range(2)]
        x_res = [sb(f"x_res{i}", [P, M, D]) for i in range(2)]
        xn = [sb(f"xn{i}", [P, M, D]) for i in range(2)]
        hT = [sb(f"hT_{s}", [P, K, N], F32R) for s in ("hi", "lo")]
        fcol_heads = [sb(f"fcol_heads{i}", [P, M, 2 * H]) for i in range(2)]
        fcol_one = {"merge": sb("fcol_merge", [P, M, 2]), "last": sb("fcol_last", [P, M, 2])}
        val = [[sb(f"val{i}_{s}", [P, M, F + H * D], F32R) for s in ("hi", "lo")] for i in range(2)]
        cat = [sb(f"cat_{s}", [P, KH, N], F32R) for s in ("hi", "lo")]
        val_merge = [sb(f"val_merge_{s}", [P, M, D], F32R) for s in ("hi", "lo")]
        gatT = [[sb(f"gatT{i}_{s}", [P, K, N], F32R) for s in ("hi", "lo")] for i in range(2)]
        ff = sb("ff", [P, K, N])
        ffT = [sb(f"ffT_{s}", [P, K, N], F32R) for s in ("hi", "lo")]
        y_scaled = sb("y_scaled", [P, M, D])
        x1 = [sb(f"x1_{i}", [P, M, D]) for i in range(2)]
        x1n = [sb(f"x1n{i}", [P, M, D]) for i in range(2)]
        h1T = [sb(f"h1T_{s}", [P, K, N], F32R) for s in ("hi", "lo")]
        val_last_both = sb("val_last", [P, M, 2 * O1], F32R)
        val_last = [val_last_both[:, :, s * O1:(s + 1) * O1] for s in range(2)]
        result = [sb(f"result{i}", [P, M, D]) for i in range(2)]
        LNS = {"x": NORM, "y": FFN, "x1": FFN}
        ln_stats = {n: sb(f"stats_{n}", [P, M, 6]) for n in LNS}
        moments = {n: sb(f"moments_{n}", [P, M, 2]) for n in LNS}
        var_eps = {n: sb(f"var_eps_{n}", [P, M]) for n in LNS}
        mean_neg = {n: sb(f"mean_neg_{n}", [P, M]) for n in LNS}
        rstd = {n: sb(f"rstd_{n}", [P, M]) for n in LNS}

        work = sb("work", [P, len(NAMES) + len(ELUS), M * N])
        probs = {n: work[:, i, :].rearrange("p (m n) -> p m n", m=M) for i, n in enumerate(NAMES)}
        elu = {n: work[:, len(NAMES) + i, :] for i, n in enumerate(ELUS)}
        probsT_two = [[sb(f"probsT{i}_{s}", [P, M, N], F32R) for s in ("hi", "lo")] for i in range(2)]
        probsT = {n: probsT_two[i % 2] for i, n in enumerate(TURNS)}
        row_min = {n: sb(f"row_min_{n}", [P, M]) for n in NAMES}
        row_sum = {n: sb(f"row_sum_{n}", [P, M]) for n in NAMES}
        row_rec = {n: sb(f"row_rec_{n}", [P, M]) for n in NAMES}

        row_made = per_unit("row_made")
        scored = per_unit("scored")
        leaked = per_unit("leaked")
        masked = per_unit("masked")
        exped = per_unit("exped")
        inverted = per_unit("inverted")
        scaled = per_unit("scaled", ELUS)
        turned = per_unit("turned")
        turned_hi = per_unit("turned_hi")
        turned_lo = per_unit("turned_lo")
        attended = per_unit("attended")
        elu_exp = per_unit("elu_exp", ELUS)
        elu_clip = per_unit("elu_clip", ELUS)
        elu_done = per_unit("elu_done", ELUS)
        elu_hi = per_unit("elu_hi", ELUS)
        elu_lo = per_unit("elu_lo", ELUS)
        ln_chain = {n: sem(f"ln_chain_{n}") for n in LNS}
        ln_rstd = {n: sem(f"ln_rstd_{n}") for n in LNS}
        x_loaded = [sem(f"x_loaded{i}") for i in range(2)]
        xn_done = sem("xn_done")
        hT_turned, hT_hi, hT_lo = sem("hT_turned"), sem("hT_hi"), sem("hT_lo")
        fcol_kept = sem("fcol_kept")
        val_made, val_hi, val_lo = sem("val_made"), sem("val_hi"), sem("val_lo")
        wo_made, wo_hi, wo_lo = sem("wo_made"), sem("wo_hi"), sem("wo_lo")
        up_made, up_relu, up_hi, up_lo = sem("up_made"), sem("up_relu"), sem("up_hi"), sem("up_lo")
        y_made, y_scaled_done, x1_done, x1n_done = sem("y_made"), sem("y_scaled_done"), sem("x1_done"), sem("x1n_done")
        res_loaded = [sem(f"res_loaded{i}") for i in range(2)]
        res_beta = sem("res_beta")
        h1T_turned, h1T_hi, h1T_lo = sem("h1T_turned"), sem("h1T_hi"), sem("h1T_lo")
        last_made, last_hi, last_lo = sem("last_made"), sem("last_hi"), sem("last_lo")
        result_left = sem("result_left")
        stored = [sem(f"stored{i}") for i in range(2)]
        loaded_heads = [sem(f"loaded_heads{k}") for k in range(K)]
        loaded_adj, loaded_out, loaded_ffn, loaded_last = sem("loaded_adj"), sem("loaded_out"), sem("loaded_ffn"), sem("loaded_last")
        constants_made = sem("constants_made")
        heads_hi, heads_lo = sem("heads_hi"), sem("heads_lo")
        late_hi, out_split, ffn_split, last_split = sem("late_hi"), sem("out_split"), sem("ffn_split"), sem("last_split")
        set_up_dve = sem("set_up_dve")
        heads_folded, out_folded, last_folded, b2_made = sem("heads_folded"), sem("out_folded"), sem("last_folded"), sem("b2_made")

        class Step:

            def __init__(self, eng, t=None, pair=None, odd=0, kept=None):
                self.eng, self.t, self.pair, self.odd, self.kept = eng, t, pair, odd, kept

            def runs(self, stage):
                return self.t is None or 0 <= self.t - stage < NB

            def parity(self, stage):
                return (self.odd - stage) % 2 if self.t is None else (self.t - stage) % 2

            def graph(self, stage):
                return 2 * self.pair + (self.odd - stage) if self.t is None else self.t - stage

            def linear(self, slope, offset):
                if (slope, offset) not in self.kept:
                    self.kept[slope, offset] = self.eng.snap(slope * self.pair + offset)
                return self.kept[slope, offset]

            def after(self, semaphore, stage, back=0, per=1, i=None):
                i = per if i is None else i
                if self.t is None:
                    return semaphore, self.linear(2 * per, per * (self.odd - stage - back) + i)
                b = self.t - stage - back
                if b < 0:
                    return constants_made, CONSTANTS
                return semaphore, per * b + i if b < NB else per * NB

            def after_dma(self, pair_of, stage, back=0):
                if self.t is None:
                    b = self.odd - stage - back
                    return pair_of[b % 2], self.linear(16, 16 * (b // 2 + 1))
                b = self.t - stage - back
                if b < 0:
                    return constants_made, CONSTANTS
                return pair_of[b % 2], 16 * (min(b, NB - 2 + b % 2) // 2 + 1)

            def freed(self, order, use):
                at = [o[0] for o in order].index(use)
                for n in range(1, STAGES * len(order)):
                    back, before = divmod(at - n, len(order))
                    _, stage, semaphore, per, i = order[before]
                    if self.t is None or 0 <= self.t - stage + back < NB:
                        return self.after(semaphore, stage, -back, per, i)
                return constants_made, CONSTANTS

        row_order = [(n, UNITS[n].stage, scored[n], 1, 1) for n in ROWS]
        turn_order = {n: [(w, UNITS[w].stage, turned_lo[w], 1, 1) for w in TURNS[i % 2::2]] for i, n in enumerate(TURNS)}
        probsT_order = {n: [(w, UNITS[w].stage, attended[w], 1, 1) for w in TURNS[i % 2::2]] for i, n in enumerate(TURNS)}
        att_order = {n: [(w, UNITS[w].stage, elu_done[w], 1, 1) if w in ELUS else (w, LAST, result_left, 2, 2)
                         for w in ATTENDS[i % 2::2]] for i, n in enumerate(ATTENDS)}
        ATTENDED_LAST = [n for n in ATTENDS if n in ("h0", "h1", "h2", "h3")][-1]
        SCORED_LAST = [n for n in ROWS if n in ("h0", "h1", "h2", "h3")][-1]
        VALS, MERGES = [[int(n[-1]) for n in PRODUCTS if n.startswith(k)] for k in ("val", "wo")]
        freed_by = {
            "h1T": (LAST, h1T_lo, 1, 1), "hT": (VALUES, hT_lo, 1, 1), "last": (LAST, last_lo, 3, 3),
            "up": (FFN, up_relu, 1, 1), "y": (FFN, y_scaled_done, 1, 1),
            **{f"val{q}": (VALUES, val_lo, CHUNKS * M, VALS.index(q) + 1) for q in range(CHUNKS * M)},
            **{f"wo{m}": (MERGE, wo_lo, 4, 2 * MERGES.index(m) + 2) for m in range(M)}}
        mm_uses = [(n, *freed_by[n]) for n in PRODUCTS]
        mm_at = {u[0]: i % 3 for i, u in enumerate(mm_uses)}
        mm_order = [mm_uses[i::3] for i in range(3)]

        def bank(use):
            return bank_mm[mm_at[use]]

        STEPS = NB + STAGES - 1
        FIRST = STAGES + STAGES % 2
        LASTP = NB // 2

        def every_step(eng, body, set_up={}):
            for t in range(FIRST):
                if t in set_up:
                    set_up[t]()
                body(Step(eng, t=t))
            with eng.Fori(FIRST // 2, LASTP) as pair:
                kept = {}
                for odd in range(2):
                    body(Step(eng, pair=pair, odd=odd, kept=kept))
            for t in range(2 * LASTP, STEPS):
                body(Step(eng, t=t))

        F_OUT = 2 * H * K
        F_LAST = F_OUT + 2 * KH
        A_OUT = 2 * H * D
        A_LAST = A_OUT + 2 * D

        raw_heads = [work[:, 2 * k:2 * (k + 1), :].rearrange("p a b -> p (a b)") for k in range(K)]
        raw_out = [work[:, NAMES.index("merge"), :], work[:, NAMES.index("last"), :],
                   elu["merge"], x1[0][:].rearrange("p m d -> p (m d)")]
        raw_up, raw_down, raw_last = (t[:].rearrange("p m d -> p (m d)") for t in (x1[1], x1n[0], x1n[1]))
        PER = KH // len(raw_out)

        def elu_from(n):
            return elu[n].rearrange("p (k n) -> p k n", k=K)

        def elu_to(s, n):
            if n == "merge":
                return [t[:] for t in gatT[s.parity(MERGE)]]
            return [t[:, K * UNITS[n].head:K * (UNITS[n].head + 1), :] for t in cat]

        def graph_rows(tensor, s, stage):
            return tensor.rearrange("b (p m) f -> b p m f", m=M)[s.graph(stage)]

        block = ctx.enter_context(nc.Block())

        @block.sync
        def _(sp):
            def load(dst, src, done):
                sp.dma_start(dst, src).then_inc(done, 16)

            def repeated(vector, width, partitions=P):
                return vector.to_broadcast([partitions, width])

            load(x_in[0][:], x.rearrange("b (p m) f -> b p m f", m=M)[0], x_loaded[0])
            heads = W_heads.rearrange("h (k p) o -> k p h o", p=P)
            load(raw_heads[0].rearrange("p (h o) -> p h o", h=H), heads[0], loaded_heads[0])
            load(a_rows[:, 0:A_OUT], repeated(a_heads.rearrange("(a h) d -> a (h d)", a=1), A_OUT), loaded_heads[0])
            for k in range(1, K):
                load(raw_heads[k].rearrange("p (h o) -> p h o", h=H), heads[k], loaded_heads[k])
            load(x_in[1][:], x.rearrange("b (p m) f -> b p m f", m=M)[1], x_loaded[1])
            load(adj_sb[:], adj.rearrange("(p m) n -> p m n", m=M), loaded_adj)
            for i, dst in enumerate(raw_out):
                load(dst.rearrange("p (k o) -> p k o", k=PER),
                     W_out.rearrange("(i k p) o -> i p k o", p=P, k=PER)[i], loaded_out)
            load(a_rows[:, A_OUT:A_LAST], repeated(a_out.rearrange("(a d) -> a d", a=1), 2 * D), loaded_out)
            for dst, w in ((raw_up, w1), (raw_down, w2)):
                load(dst.rearrange("p (k o) -> p k o", k=K), w.rearrange("(k p) o -> p k o", p=P), loaded_ffn)
            load(b2_rows[:], repeated(b2.rearrange("(a d) -> a d", a=1), D, 2), loaded_ffn)
            load(gamma_rows[:], repeated(gamma.rearrange("(a d) -> a d", a=1), D), loaded_ffn)
            load(beta_rows[:, 0, :], repeated(beta.rearrange("(a d) -> a d", a=1), D), loaded_ffn)
            with nc.allow_non_contiguous_dma(reason="256 values, once"):
                load(b1_col[:], b1.rearrange("(k p) -> p k", p=P), loaded_ffn)
            load(raw_last[:, 0:K * O1].rearrange("p (k o) -> p k o", k=K),
                 W_last.rearrange("(k p) o -> p k o", p=P), loaded_last)
            load(a_rows[:, A_LAST:], repeated(a_last.rearrange("s o (a) -> a (s o)", a=1), 2 * O1), loaded_last)

            def step(s):
                if s.runs(FFN - 1):
                    sp.wait_ge(*s.after(x1_done, FFN - 1, back=2))
                    par = s.parity(FFN - 1)
                    sp.dma_start(x_res[par][:], graph_rows(x, s, FFN - 1)).then_inc(res_loaded[par], 16)
                if s.t is None or s.t + 2 < NB:
                    sp.wait_ge(*s.after(xn_done, NORM))
                    par = s.parity(NORM)
                    sp.dma_start(x_in[par][:], graph_rows(x, s, NORM - 2)).then_inc(x_loaded[par], 16)
                if s.runs(LAST):
                    sp.wait_ge(*s.after(result_left, LAST, per=2))
                    par = s.parity(LAST)
                    sp.dma_start(graph_rows(out, s, LAST), result[par][:]).then_inc(stored[par], 16)

            for t in range(FIRST):
                step(Step(sp, t=t))
            with sp.Fori(FIRST // 2, LASTP - 1) as pair:
                kept = {}
                for odd in range(2):
                    step(Step(sp, pair=pair, odd=odd, kept=kept))
            for t in range(2 * LASTP - 2, STEPS):
                step(Step(sp, t=t))
            for par in range(2):
                sp.wait_ge(stored[par], 16 * (NB // 2))

        @block.gpsimd
        def _(pool):
            nc.gpsimd.memset(ident[:], 0.0).then_inc(constants_made, 1)
            nc.gpsimd.memset(half_neg[:], -0.5).then_inc(constants_made, 1)
            nc.gpsimd.memset(b2_keep[:], -1.0).then_inc(constants_made, 1)
            pool.wait_ge(constants_made, 3)
            nc.gpsimd.affine_select(out=ident[:], in_=ident[:], compare_op=ALU.not_equal, fill=1.0, base=0,
                                    pattern=[[-1, P]], channel_multiplier=1).then_inc(constants_made, 1)
            nc.gpsimd.memset(b2_keep[0:1, :], 0.0).then_inc(constants_made, 1)

            def low_part(src, pair, finished):
                nc.gpsimd.tensor_tensor(pair[1], src, pair[0].bitcast(F32), ALU.subtract).then_inc(finished, 1)

            def split_heads():
                for k in range(K):
                    pool.wait_ge(heads_hi, k + 1)
                    low_part(raw_heads[k], [w[:, k, F:] for w in Wv], heads_lo)

            def split_late():
                for i, src in enumerate(raw_out):
                    pool.wait_ge(late_hi, i + 1)
                    low_part(src.rearrange("p (k o) -> p k o", k=PER), [w[:, PER * i:PER * (i + 1), 0:D] for w in Wo], out_split)
                late = len(raw_out)
                for i, (src, pair) in enumerate(((raw_up, Wu), (raw_down, Wd))):
                    pool.wait_ge(late_hi, late + i + 1)
                    low_part(src.rearrange("p (k o) -> p k o", k=K), [w[:] for w in pair], ffn_split)
                pool.wait_ge(late_hi, late + 3)
                low_part(raw_last[:, 0:K * O1].rearrange("p (k o) -> p k o", k=K), [w[:, :, 0:O1] for w in Wl], last_split)

            def rsqrt(s, n):
                if not s.runs(LNS[n]):
                    return
                pool.wait_ge(*s.after(ln_chain[n], LNS[n], per=3))
                nc.gpsimd.tensor_tensor(rstd[n][:], var_eps[n][:], half_neg[:], ALU.pow).then_inc(ln_rstd[n], 1)

            def normalise(s, n, src, dst, done):
                pool.wait_ge(*s.after(ln_rstd[n], LNS[n]))
                pool.nop(nofuse=True)
                for m in range(M):
                    last = nc.gpsimd.tensor_scalar(dst[:, m, :], src[:, m, :], mean_neg[n][:, m:m + 1],
                                                   rstd[n][:, m:m + 1], ALU.add, ALU.mult)
                last.then_inc(done, 1)

            def norm_x(s):
                if not s.runs(NORM):
                    return
                pool.wait_ge(*s.after(hT_turned, NORM, back=2))
                normalise(s, "x", x_in[s.parity(NORM)], xn[s.parity(NORM)], xn_done)

            def norm_x1(s):
                if not s.runs(FFN):
                    return
                pool.wait_ge(*s.after(h1T_turned, FFN, back=2))
                normalise(s, "x1", x1[s.parity(FFN)], x1n[s.parity(FFN)], x1n_done)

            def residual(s):
                if not s.runs(FFN):
                    return
                pool.wait_ge(*s.after_dma(res_loaded, FFN))
                if s.t == FFN:
                    pool.wait_ge(loaded_ffn, 16 * 6)
                par = s.parity(FFN)
                nc.gpsimd.tensor_tensor(x_res[par][:], x_res[par][:], beta_rows[:].to_broadcast([P, M, D]),
                                        ALU.add).then_inc(res_beta, 1)

            def ffn_hi(s):
                if not s.runs(FFN):
                    return
                pool.wait_ge(*s.after(up_relu, FFN))
                pool.wait_ge(*s.after(y_made, FFN, back=1))
                pool.nop(nofuse=True)
                nc.gpsimd.tensor_scalar(ffT[0][:], ff[:], 1.0, 0.0, ALU.mult, ALU.add).then_inc(up_hi, 1)

            def scale(s, n):
                u = UNITS[n]
                if not s.runs(u.stage):
                    return
                pool.wait_ge(*s.after(inverted[n], u.stage))
                pool.nop(nofuse=True)
                for m in range(M):
                    last = nc.gpsimd.tensor_scalar(probs[n][:, m, :], probs[n][:, m, :], row_rec[n][:, m:m + 1],
                                                   1.0, ALU.mult, ALU.mult)
                last.then_inc(scaled[n], 1)

            def split_hi(s, n):
                u = UNITS[n]
                if not s.runs(u.stage):
                    return
                pool.wait_ge(*s.after(elu_done[n], u.stage))
                if n == "merge":
                    pool.wait_ge(*s.after(up_made, MERGE, back=2))
                    pool.nop(nofuse=True)
                else:
                    pool.wait_ge(*s.after(wo_made, HEADS, back=1, per=2))
                    pool.nop(nofuse=True)
                nc.gpsimd.tensor_scalar(elu_to(s, n)[0], elu_from(n), 1.0, 0.0, ALU.mult, ALU.add).then_inc(elu_hi[n], 1)

            def split_lo(s, n):
                u = UNITS[n]
                if not s.runs(u.stage):
                    return
                hi, lo = elu_to(s, n)
                pool.wait_ge(*s.after(elu_hi[n], u.stage))
                nc.gpsimd.tensor_tensor(lo, elu_from(n), hi.bitcast(F32), ALU.subtract).then_inc(elu_lo[n], 1)

            def step(s):
                residual(s)
                scale(s, "h0")
                ffn_hi(s)
                scale(s, "h1")
                scale(s, "h2")
                rsqrt(s, "x")
                split_hi(s, "h0")
                scale(s, "merge")
                split_lo(s, "h0")
                rsqrt(s, "y")
                scale(s, "h3")
                split_hi(s, "h1")
                split_hi(s, "h2")
                split_lo(s, "h2")
                split_lo(s, "h1")
                split_hi(s, "merge")
                split_lo(s, "merge")
                split_hi(s, "h3")
                split_lo(s, "h3")
                rsqrt(s, "x1")
                norm_x(s)
                norm_x1(s)

            pool.wait_ge(constants_made, CONSTANTS)
            every_step(pool, step, {1: split_heads, 2: split_late})

        @block.scalar
        def _(act):
            def hi_copy(dst, src, done, func=ACT.Identity):
                nc.scalar.activation(dst, src, func).then_inc(done, 1)

            def scores(s, n):
                u = UNITS[n]
                if not s.runs(u.stage):
                    return
                act.wait_ge(*s.after(row_made[n], u.stage))
                act.wait_ge(*s.after(turned[n], u.stage, back=1))
                col = fcol_heads[s.parity(HEADS)] if u.stage == HEADS else fcol_one[n]
                for m in range(M):
                    last = nc.scalar.activation(probs[n][:, m, :], bank_row[:, 0:N], ACT.Identity,
                                                bias=col[:, m, u.head:u.head + 1])
                last.then_inc(scored[n], 1)

            def exps(s, n):
                u = UNITS[n]
                if not s.runs(u.stage):
                    return
                act.wait_ge(*s.after(masked[n], u.stage))
                for m in range(M):
                    last = nc.scalar.activation(probs[n][:, m, :], probs[n][:, m, :], ACT.Exp, scale=-1.0,
                                                bias=row_min[n][:, m:m + 1], accum_out=row_sum[n][:, m:m + 1])
                last.then_inc(exped[n], 1)

            def turn_hi(s, n):
                u = UNITS[n]
                if not s.runs(u.stage):
                    return
                act.wait_ge(*s.after(turned[n], u.stage))
                act.wait_ge(*s.freed(probsT_order[n], n))
                hi_copy(probsT[n][0][:].rearrange("p m n -> p (m n)"), bank_turn[n], turned_hi[n])

            def elu_exps(s, n):
                u = UNITS[n]
                if not s.runs(u.stage):
                    return
                act.wait_ge(*s.after(attended[n], u.stage))
                act.wait_ge(*s.after(elu_lo[n], u.stage, back=1))
                if n == "merge":
                    act.wait_ge(*s.after(y_made, MERGE, back=1))
                nc.scalar.activation(elu[n], bank_att[n], ACT.Exp).then_inc(elu_exp[n], 1)

            def clip(s, n):
                u = UNITS[n]
                if not s.runs(u.stage):
                    return
                act.wait_ge(*s.after(elu_exp[n], u.stage))
                nc.scalar.activation(elu[n], elu[n], ACT.Relu, bias=1.0, scale=-1.0).then_inc(elu_clip[n], 1)

            def turn_x(s):
                if not s.runs(VALUES):
                    return
                act.wait_ge(*s.after(hT_turned, VALUES))
                act.wait_ge(*s.after(val_made, VALUES, back=1, per=CHUNKS * M))
                hi_copy(hT[0][:].rearrange("p k n -> p (k n)"), bank("hT"), hT_hi, ACT.Relu)

            def value_hi(s, q):
                if not s.runs(VALUES):
                    return
                m, c = divmod(q, CHUNKS)
                act.wait_ge(*s.after(val_made, VALUES, per=CHUNKS * M, i=VALS.index(q) + 1))
                act.wait_ge(*s.after(attended[ATTENDED_LAST], HEADS + 1))
                hi_copy(val[s.parity(VALUES)][0][:, m, c * VW:(c + 1) * VW], bank(f"val{q}")[:, 0:VW], val_hi)

            def merge_hi(s, m):
                if not s.runs(MERGE):
                    return
                act.wait_ge(*s.after(wo_made, MERGE, per=2, i=MERGES.index(m) + 1))
                act.wait_ge(*s.after(attended["merge"], MERGE, back=1))
                hi_copy(val_merge[0][:, m, :], bank(f"wo{m}")[:, 0:D], wo_hi)

            def ffn_relu(s):
                if not s.runs(FFN):
                    return
                act.wait_ge(*s.after(up_made, FFN))
                act.wait_ge(*s.after(up_lo, FFN, back=1))
                for k in range(K):
                    last = nc.scalar.activation(ff[:, k, :], bank("up")[:, k * N:(k + 1) * N], ACT.Relu,
                                                bias=b1_col[:, k:k + 1])
                last.then_inc(up_relu, 1)

            def turn_x1(s):
                if not s.runs(LAST):
                    return
                act.wait_ge(*s.after(h1T_turned, LAST))
                act.wait_ge(*s.after(last_made, LAST, back=1))
                hi_copy(h1T[0][:].rearrange("p k n -> p (k n)"), bank("h1T"), h1T_hi, ACT.Relu)

            def last_hi_copy(s):
                if not s.runs(LAST):
                    return
                act.wait_ge(*s.after(last_made, LAST))
                act.wait_ge(*s.after(attended["last"], LAST, back=1))
                hi_copy(val_last[0], bank("last").rearrange("p (m o) -> p m o", m=M)[:, :, 0:O1], last_hi)

            def step(s):
                scores(s, "h0")
                ffn_relu(s)
                scores(s, "h1")
                exps(s, "h0")
                scores(s, "h2")
                merge_hi(s, 1)
                exps(s, "h1")
                merge_hi(s, 0)
                turn_hi(s, "h0")
                turn_x(s)
                turn_x1(s)
                turn_hi(s, "h1")
                scores(s, "merge")
                exps(s, "h2")
                elu_exps(s, "h0")
                clip(s, "h0")
                scores(s, "h3")
                exps(s, "merge")
                last_hi_copy(s)
                turn_hi(s, "h2")
                value_hi(s, 0)
                exps(s, "h3")
                elu_exps(s, "h1")
                scores(s, "last")
                clip(s, "h1")
                turn_hi(s, "merge")
                elu_exps(s, "h2")
                value_hi(s, 2)
                clip(s, "h2")
                turn_hi(s, "h3")
                value_hi(s, 4)
                exps(s, "last")
                value_hi(s, 1)
                elu_exps(s, "merge")
                turn_hi(s, "last")
                clip(s, "merge")
                elu_exps(s, "h3")
                clip(s, "h3")
                value_hi(s, 3)
                value_hi(s, 5)

            def high_heads():
                for k in range(K):
                    act.wait_ge(loaded_heads[k], 16 * (2 if k == 0 else 1))
                    hi_copy(Wv[0][:, k, F:], raw_heads[k], heads_hi)

            def high_late():
                act.wait_ge(loaded_out, 16 * (len(raw_out) + 1))
                for i, src in enumerate(raw_out):
                    hi_copy(Wo[0][:, PER * i:PER * (i + 1), 0:D], src.rearrange("p (k o) -> p k o", k=PER), late_hi)
                act.wait_ge(loaded_ffn, 16 * 6)
                hi_copy(Wu[0][:], raw_up.rearrange("p (k o) -> p k o", k=K), late_hi)
                hi_copy(Wd[0][:], raw_down.rearrange("p (k o) -> p k o", k=K), late_hi)
                act.wait_ge(loaded_last, 32)
                hi_copy(Wl[0][:, :, 0:O1], raw_last[:, 0:K * O1].rearrange("p (k o) -> p k o", k=K), late_hi)

            act.wait_ge(constants_made, CONSTANTS)
            every_step(act, step, {1: high_heads, 2: high_late})

        @block.vector
        def _(dve):
            done = [0]

            def chained(instruction):
                done[0] += 1
                instruction.then_inc(set_up_dve, 1)

            unused = [t[:, m, :] for t in (y_scaled, result[0], result[1], ff) for m in range(M)]
            folded = []

            def fold_vector(w, a, dst, width):
                if len(folded) >= len(unused):
                    dve.wait_ge(set_up_dve, folded[-len(unused)])
                chained(nc.vector.tensor_tensor_reduce(unused[len(folded) % len(unused)][:, 0:width], w, a, -1.0, 0.0,
                                                       ALU.mult, ALU.add, dst))
                folded.append(done[0])

            def split_folds(pair, columns, finished):
                hi, lo = pair
                dve.wait_ge(set_up_dve, done[0])
                chained(nc.vector.tensor_copy(hi, columns))
                dve.wait_ge(set_up_dve, done[0])
                nc.vector.tensor_tensor(lo, columns, hi.bitcast(F32), ALU.subtract).then_inc(finished, 1)

            def fold_heads():
                for k in range(K):
                    dve.wait_ge(loaded_heads[k], 16 * (2 if k == 0 else 1))
                    for h in range(H):
                        for side in range(2):
                            at = 2 * H * k + side * H + h
                            fold_vector(raw_heads[k][:, h * D:(h + 1) * D],
                                        a_rows[:, (2 * h + side) * D:(2 * h + side + 1) * D], fold[:, at:at + 1], D)
                split_folds([w[:, :, 0:F] for w in Wv], fold[:, 0:F_OUT].rearrange("p (k f) -> p k f", k=K), heads_folded)

            def make_masks():
                dve.wait_ge(loaded_adj, 16)
                keys = adj_sb[:].rearrange("p m (q w) -> p m w q", w=M)
                for m in range(M):
                    chained(nc.vector.tensor_scalar(mask_first[:, m, :].rearrange("p (w q) -> p w q", w=M), keys[:, m],
                                                    0.0, BIG, ALU.is_le, ALU.mult))
                    chained(nc.vector.tensor_scalar(mask_last[:, m, :].rearrange("p (w q) -> p w q", w=M), keys[:, m],
                                                    -NEG, NEG, ALU.mult, ALU.add))
                dve.wait_ge(set_up_dve, done[0])

            def fold_late():
                dve.wait_ge(loaded_out, 16 * (len(raw_out) + 1))
                for k in range(KH):
                    i, j = divmod(k, PER)
                    for side in range(2):
                        fold_vector(raw_out[i][:, j * D:(j + 1) * D], a_rows[:, A_OUT + side * D:A_OUT + (side + 1) * D],
                                    fold[:, F_OUT + 2 * k + side:F_OUT + 2 * k + side + 1], D)
                split_folds([w[:, :, D:D + 2] for w in Wo], fold[:, F_OUT:F_LAST].rearrange("p (k s) -> p k s", s=2), out_folded)
                dve.wait_ge(loaded_last, 32)
                for k in range(K):
                    for side in range(2):
                        fold_vector(raw_last[:, k * O1:(k + 1) * O1], a_rows[:, A_LAST + side * O1:A_LAST + (side + 1) * O1],
                                    fold[:, F_LAST + 2 * k + side:F_LAST + 2 * k + side + 1], O1)
                split_folds([w[:, :, O1:O1 + 2] for w in Wl], fold[:, F_LAST:].rearrange("p (k s) -> p k s", s=2), last_folded)
                dve.wait_ge(loaded_ffn, 16 * 6)
                chained(nc.vector.tensor_copy(b2_split[:], b2_rows[:]))
                chained(nc.vector.tensor_scalar(ones2[:], ident[0:2, :], 0.0, 1.0, ALU.mult, ALU.add))
                dve.wait_ge(set_up_dve, done[0])
                nc.vector.scalar_tensor_tensor(out=b2_split[:], in0=b2_split[:].bitcast(F32), scalar=b2_keep[:, 0:1],
                                               in1=b2_rows[:], op0=ALU.mult, op1=ALU.add).then_inc(b2_made, 1)
                dve.wait_ge(set_up_dve, done[0])

            def stats(s, n, src):
                dve.wait_ge(*s.after(ln_rstd[n], LNS[n], back=1))
                dve.wait_ge(*s.after({"x": xn_done, "y": x1_done, "x1": x1n_done}[n], LNS[n], back=1))
                for m in range(M):
                    last = nc.vector.bn_stats(ln_stats[n][:, m, :], src(m))
                last.then_inc(ln_chain[n], 1)

            def aggregate(s, n):
                if not s.runs(LNS[n]):
                    return
                dve.wait_ge(*s.after(ln_chain[n], LNS[n], per=3, i=1))
                dve.nop(nofuse=True)
                for m in range(M):
                    last = nc.vector.bn_aggr(moments[n][:, m, :], ln_stats[n][:, m, :])
                last.then_inc(ln_chain[n], 1)

            def mean_and_var(s, n):
                if not s.runs(LNS[n]):
                    return
                dve.wait_ge(*s.after(ln_chain[n], LNS[n], per=3, i=2))
                nc.vector.tensor_scalar(mean_neg[n][:], moments[n][:, :, 0], -1.0, None, ALU.mult)
                nc.vector.tensor_scalar(var_eps[n][:], moments[n][:, :, 1], LN_EPS, None, ALU.add).then_inc(ln_chain[n], 1)

            def stats_x(s):
                if s.runs(NORM):
                    dve.wait_ge(*s.after_dma(x_loaded, NORM))
                    stats(s, "x", lambda m: x_in[s.parity(NORM)][:, m, :])

            def stats_y(s):
                if s.runs(FFN):
                    dve.wait_ge(*s.after(y_made, FFN))
                    stats(s, "y", lambda m: bank("y")[:, m * D:(m + 1) * D])

            def stats_x1(s):
                if s.runs(FFN):
                    dve.wait_ge(*s.after(x1_done, FFN))
                    stats(s, "x1", lambda m: x1[s.parity(FFN)][:, m, :])

            def leak(s, n):
                u = UNITS[n]
                if not s.runs(u.stage):
                    return
                dve.wait_ge(*s.after(scored[n], u.stage))
                nc.vector.scalar_tensor_tensor(out=probs[n], in0=probs[n], scalar=u.slope, in1=probs[n],
                                               op0=ALU.mult, op1=ALU.min).then_inc(leaked[n], 1)

            def mask_and_min(s, n):
                u = UNITS[n]
                if not s.runs(u.stage):
                    return
                dve.wait_ge(*s.after(leaked[n], u.stage))
                dve.nop(nofuse=True)
                mask = mask_last if n == "last" else mask_first
                for m in range(M):
                    last = nc.vector.tensor_tensor_reduce(probs[n][:, m, :], probs[n][:, m, :], mask[:, m, :],
                                                          1.0, 3e38, ALU.add, ALU.min, row_min[n][:, m:m + 1])
                last.then_inc(masked[n], 1)

            def invert(s, n):
                u = UNITS[n]
                if not s.runs(u.stage):
                    return
                dve.wait_ge(*s.after(exped[n], u.stage))
                nc.vector.reciprocal(row_rec[n][:], row_sum[n][:]).then_inc(inverted[n], 1)

            def turn_lo(s, n):
                u = UNITS[n]
                if not s.runs(u.stage):
                    return
                hi, lo = (t[:].rearrange("p m n -> p (m n)") for t in probsT[n])
                dve.wait_ge(*s.after(turned_hi[n], u.stage))
                nc.vector.tensor_tensor(lo, bank_turn[n], hi.bitcast(F32), ALU.subtract).then_inc(turned_lo[n], 1)

            def elus(s, n):
                u = UNITS[n]
                if not s.runs(u.stage):
                    return
                dve.wait_ge(*s.after(elu_clip[n], u.stage))
                nc.vector.scalar_tensor_tensor(out=elu[n], in0=elu[n], scalar=-1.0, in1=bank_att[n],
                                               op0=ALU.mult, op1=ALU.max).then_inc(elu_done[n], 1)

            def relu_lo(pair, src, finished):
                hi, lo = (t[:].rearrange("p k n -> p (k n)") for t in pair)
                nc.vector.scalar_tensor_tensor(out=lo, in0=src, scalar=0.0, in1=hi.bitcast(F32),
                                               op0=ALU.max, op1=ALU.subtract).then_inc(finished, 1)

            def turn_x(s):
                if s.runs(VALUES):
                    dve.wait_ge(*s.after(hT_hi, VALUES))
                    relu_lo(hT, bank("hT"), hT_lo)

            def value_lo(s, q):
                if not s.runs(VALUES):
                    return
                m, c = divmod(q, CHUNKS)
                hi, lo = (t[:, m, c * VW:(c + 1) * VW] for t in val[s.parity(VALUES)])
                dve.wait_ge(*s.after(val_hi, VALUES, per=CHUNKS * M, i=VALS.index(q) + 1))
                if c == 0:
                    dve.wait_ge(*s.after(scored[SCORED_LAST], HEADS + 1))
                    nc.vector.tensor_copy(fcol_heads[s.parity(VALUES)][:, m, :], bank(f"val{q}")[:, 0:F]).then_inc(fcol_kept, 1)
                nc.vector.tensor_tensor(lo, bank(f"val{q}")[:, 0:VW], hi.bitcast(F32), ALU.subtract).then_inc(val_lo, 1)

            def merge_lo(s, m):
                if not s.runs(MERGE):
                    return
                hi, lo = (t[:, m, :] for t in val_merge)
                dve.wait_ge(*s.after(wo_hi, MERGE, per=2, i=MERGES.index(m) + 1))
                nc.vector.tensor_tensor(lo, bank(f"wo{m}")[:, 0:D], hi.bitcast(F32), ALU.subtract).then_inc(wo_lo, 1)
                dve.wait_ge(*s.after(scored["merge"], MERGE, back=1))
                nc.vector.tensor_copy(fcol_one["merge"][:, m, :], bank(f"wo{m}")[:, D:D + 2]).then_inc(wo_lo, 1)

            def ffn_lo(s):
                if not s.runs(FFN):
                    return
                dve.wait_ge(*s.after(up_hi, FFN))
                nc.vector.tensor_tensor(ffT[1][:], ff[:], ffT[0][:].bitcast(F32), ALU.subtract).then_inc(up_lo, 1)

            def scale_y(s):
                if not s.runs(FFN):
                    return
                dve.wait_ge(*s.after(ln_chain["y"], FFN, per=3, i=2))
                for m in range(M):
                    last = nc.vector.scalar_tensor_tensor(out=y_scaled[:, m, :], in0=bank("y")[:, m * D:(m + 1) * D],
                                                          scalar=moments["y"][:, m, 0:1], in1=gamma_rows[:],
                                                          op0=ALU.subtract, op1=ALU.mult)
                last.then_inc(y_scaled_done, 1)

            def make_x1(s):
                if not s.runs(FFN):
                    return
                par = s.parity(FFN)
                dve.wait_ge(*s.after(y_scaled_done, FFN))
                dve.wait_ge(*s.after(ln_rstd["y"], FFN))
                dve.wait_ge(*s.after(res_beta, FFN))
                dve.wait_ge(*s.after(result_left, FFN, back=2, per=2))
                for m in range(M):
                    last = nc.vector.scalar_tensor_tensor(out=x1[par][:, m, :], in0=y_scaled[:, m, :],
                                                          scalar=rstd["y"][:, m:m + 1], in1=x_res[par][:, m, :],
                                                          op0=ALU.mult, op1=ALU.add)
                last.then_inc(x1_done, 1)

            def turn_x1(s):
                if s.runs(LAST):
                    dve.wait_ge(*s.after(h1T_hi, LAST))
                    relu_lo(h1T, bank("h1T"), h1T_lo)

            def last_parts(s):
                if not s.runs(LAST):
                    return
                par = s.parity(LAST)
                hp = bank("last").rearrange("p (m o) -> p m o", m=M)
                dve.wait_ge(*s.after(last_hi, LAST))
                nc.vector.tensor_tensor(val_last[1], hp[:, :, 0:O1], val_last[0].bitcast(F32),
                                        ALU.subtract).then_inc(last_lo, 1)
                dve.wait_ge(*s.after(scored["last"], LAST, back=1))
                nc.vector.tensor_copy(fcol_one["last"][:], hp[:, :, O1:O1 + 2]).then_inc(last_lo, 1)
                dve.wait_ge(*s.after_dma(stored, LAST, back=2))
                nc.vector.tensor_tensor(result[par][:, :, O1:D], hp[:, :, 0:O1], x1[par][:, :, O1:D],
                                        ALU.add).then_inc(last_lo, 1)

            def last_result(s):
                if not s.runs(LAST):
                    return
                par = s.parity(LAST)
                dve.wait_ge(*s.after(attended["last"], LAST))
                for part, added in ((1, x1[par]), (0, result[par])):
                    if part == 0:
                        dve.wait_ge(*s.after(result_left, LAST, per=2, i=1))
                    for m in range(M):
                        o = (2 * m + part) * O1
                        last = nc.vector.scalar_tensor_tensor(out=result[par][:, m, 0:O1], in0=bank_att["last"][:, o:o + O1],
                                                              scalar=row_rec["last"][:, m:m + 1], in1=added[:, m, 0:O1],
                                                              op0=ALU.mult, op1=ALU.add)
                    last.then_inc(result_left, 1)

            def step(s):
                leak(s, "h0")
                mask_and_min(s, "h0")
                stats_x(s)
                leak(s, "h1")
                mask_and_min(s, "h1")
                aggregate(s, "x")
                invert(s, "h0")
                leak(s, "h2")
                merge_lo(s, 1)
                invert(s, "h1")
                mask_and_min(s, "h2")
                merge_lo(s, 0)
                turn_lo(s, "h0")
                ffn_lo(s)
                turn_x(s)
                turn_lo(s, "h1")
                mean_and_var(s, "x")
                leak(s, "merge")
                turn_x1(s)
                mask_and_min(s, "merge")
                invert(s, "h2")
                elus(s, "h0")
                stats_y(s)
                leak(s, "h3")
                aggregate(s, "y")
                mask_and_min(s, "h3")
                invert(s, "merge")
                last_parts(s)
                turn_lo(s, "h2")
                scale_y(s)
                mean_and_var(s, "y")
                invert(s, "h3")
                leak(s, "last")
                elus(s, "h1")
                value_lo(s, 0)
                mask_and_min(s, "last")
                turn_lo(s, "merge")
                elus(s, "h2")
                turn_lo(s, "h3")
                make_x1(s)
                value_lo(s, 2)
                stats_x1(s)
                invert(s, "last")
                value_lo(s, 4)
                elus(s, "merge")
                value_lo(s, 1)
                turn_lo(s, "last")
                elus(s, "h3")
                value_lo(s, 3)
                value_lo(s, 5)
                aggregate(s, "x1")
                last_result(s)
                mean_and_var(s, "x1")

            dve.wait_ge(constants_made, CONSTANTS)
            every_step(dve, step, {1: fold_heads, 2: make_masks, 3: fold_late})

        @block.tensor
        def _(pe):
            def three(out_ap, lhs, rhs, first, final):
                passes = ((lhs[0], rhs[1]), (lhs[1], rhs[0]), (lhs[0], rhs[0]))
                for i, (l, r) in enumerate(passes):
                    ins = nc.tensor.matmul(out_ap, l, r, start=first and i == 0, stop=final and i == 2)
                return ins

            def row(s, n):
                u = UNITS[n]
                if not s.runs(u.stage):
                    return
                if u.stage == HEADS:
                    pe.wait_ge(*s.after(fcol_kept, HEADS, per=M))
                    col, at = fcol_heads[s.parity(HEADS)], H + u.head
                else:
                    pe.wait_ge(*s.after(wo_lo if n == "merge" else last_lo, u.stage, per=4 if n == "merge" else 3, i=None if n == "merge" else 2))
                    col, at = fcol_one[n], 1
                pe.wait_ge(*s.freed(row_order, n))
                for m in range(M):
                    last = nc.tensor.transpose(bank_row[:, m * P:(m + 1) * P],
                                               col[:, m, at:at + 1].to_broadcast([P, P]), ident[:])
                last.then_inc(row_made[n], 1)

            def turn(s, n):
                u = UNITS[n]
                if not s.runs(u.stage):
                    return
                if n == "last":
                    pe.wait_ge(*s.after(exped[n], u.stage))
                else:
                    pe.wait_ge(*s.after(scaled[n], u.stage))
                pe.wait_ge(*s.freed(turn_order[n], n))
                for m in range(M):
                    for j in range(M):
                        last = nc.tensor.transpose(bank_turn[n][:, j * N + m * P:j * N + (m + 1) * P],
                                                   probs[n][:, m, j * P:(j + 1) * P], ident[:])
                last.then_inc(turned[n], 1)

            def attend(s, n):
                u = UNITS[n]
                if not s.runs(u.stage):
                    return
                pe.wait_ge(*s.after(turned_lo[n], u.stage))
                if u.stage == HEADS:
                    pe.wait_ge(*s.after(val_lo, HEADS, per=CHUNKS * M))
                pe.wait_ge(*s.freed(att_order[n], n))
                to = bank_att[n]
                pT = probsT[n]
                if n == "last":
                    for m in range(M):
                        for j in range(M):
                            p_hi, p_lo = (t[:, j, m * P:(m + 1) * P] for t in pT)
                            nc.tensor.matmul(to[:, 2 * m * O1:2 * (m + 1) * O1], p_hi, val_last_both[:, j, :],
                                             start=j == 0, stop=False)
                            last = nc.tensor.matmul(to[:, 2 * m * O1:(2 * m + 1) * O1], p_lo, val_last[0][:, j, :],
                                                    start=False, stop=j == M - 1)
                else:
                    v = val[s.parity(HEADS)] if u.stage == HEADS else val_merge
                    for k in range(K):
                        c = (F if u.stage == HEADS else 0) + u.head * D + k * P
                        for j in range(M):
                            last = three(to[:, k * N:(k + 1) * N], [t[:, j, c:c + P] for t in v],
                                         [t[:, j, :] for t in pT], j == 0, j == M - 1)
                last.then_inc(attended[n], 1)

            def turn_nodes(use, src, finished):
                for k in range(K):
                    for m in range(M):
                        last = nc.tensor.transpose(bank(use)[:, k * N + m * P:k * N + (m + 1) * P],
                                                   src[:, m, k * P:(k + 1) * P], ident[:])
                last.then_inc(finished, 1)

            def turn_x(s):
                if not s.runs(VALUES):
                    return
                pe.wait_ge(*s.after(xn_done, VALUES))
                pe.wait_ge(*s.freed(mm_order[mm_at["hT"]], "hT"))
                turn_nodes("hT", xn[s.parity(VALUES)], hT_turned)

            def values(s, q):
                if not s.runs(VALUES):
                    return
                m, c = divmod(q, CHUNKS)
                pe.wait_ge(*s.after(hT_lo, VALUES))
                if s.t == VALUES:
                    pe.wait_ge(heads_lo, K)
                    pe.wait_ge(heads_folded, 1)
                pe.wait_ge(*s.freed(mm_order[mm_at[f"val{q}"]], f"val{q}"))
                for k in range(K):
                    last = three(bank(f"val{q}")[:, 0:VW], [t[:, k, m * P:(m + 1) * P] for t in hT],
                                 [w[:, k, c * VW:(c + 1) * VW] for w in Wv], k == 0, k == K - 1)
                last.then_inc(val_made, 1)

            def merge(s, m):
                if not s.runs(MERGE):
                    return
                for n in ("h0", "h1", "h2", "h3"):
                    pe.wait_ge(*s.after(elu_lo[n], MERGE))
                if s.t == MERGE:
                    pe.wait_ge(out_split, len(raw_out))
                    pe.wait_ge(out_folded, 1)
                pe.wait_ge(*s.freed(mm_order[mm_at[f"wo{m}"]], f"wo{m}"))
                for c in range(KH):
                    last = three(bank(f"wo{m}")[:, 0:D + 2], [t[:, c, m * P:(m + 1) * P] for t in cat],
                                 [w[:, c, :] for w in Wo], c == 0, c == KH - 1)
                last.then_inc(wo_made, 1)

            def ffn_up(s):
                if not s.runs(FFN):
                    return
                g = gatT[s.parity(FFN)]
                pe.wait_ge(*s.after(elu_lo["merge"], FFN))
                if s.t == FFN:
                    pe.wait_ge(ffn_split, 2)
                    pe.wait_ge(b2_made, 1)
                pe.wait_ge(*s.freed(mm_order[mm_at["up"]], "up"))
                for d in range(K):
                    for k in range(K):
                        last = three(bank("up")[:, d * N:(d + 1) * N], [w[:, k, d * P:(d + 1) * P] for w in Wu],
                                     [t[:, k, :] for t in g], k == 0, k == K - 1)
                last.then_inc(up_made, 1)

            def ffn_down(s):
                if not s.runs(FFN):
                    return
                pe.wait_ge(*s.after(up_lo, FFN))
                pe.wait_ge(*s.freed(mm_order[mm_at["y"]], "y"))
                for m in range(M):
                    nodes = slice(m * P, (m + 1) * P)
                    to = bank("y")[:, m * D:(m + 1) * D]
                    for k in range(K):
                        nc.tensor.matmul(to[:, k * P:(k + 1) * P], elu_from("merge")[:, k, nodes], ident[:],
                                         is_transpose=True, start=k == 0, stop=False)
                    nc.tensor.matmul(to, ones2[:], b2_split[:], start=False, stop=False)
                    for k in range(K):
                        last = three(to, [t[:, k, nodes] for t in ffT], [w[:, k, :] for w in Wd], False, k == K - 1)
                last.then_inc(y_made, 1)

            def turn_x1(s):
                if not s.runs(LAST):
                    return
                pe.wait_ge(*s.after(x1n_done, LAST))
                pe.wait_ge(*s.freed(mm_order[mm_at["h1T"]], "h1T"))
                turn_nodes("h1T", x1n[s.parity(LAST)], h1T_turned)

            def last_values(s):
                if not s.runs(LAST):
                    return
                pe.wait_ge(*s.after(h1T_lo, LAST))
                if s.t == LAST:
                    pe.wait_ge(last_split, 1)
                    pe.wait_ge(last_folded, 1)
                pe.wait_ge(*s.freed(mm_order[mm_at["last"]], "last"))
                for m in range(M):
                    for k in range(K):
                        last = three(bank("last")[:, m * 256:m * 256 + O1 + 2], [t[:, k, m * P:(m + 1) * P] for t in h1T],
                                     [w[:, k, :] for w in Wl], k == 0, k == K - 1)
                last.then_inc(last_made, 1)

            def step(s):
                row(s, "h0")
                ffn_up(s)
                row(s, "h1")
                merge(s, 1)
                row(s, "h2")
                merge(s, 0)
                turn(s, "h0")
                turn_x(s)
                turn_x1(s)
                row(s, "merge")
                turn(s, "h1")
                attend(s, "h0")
                ffn_down(s)
                row(s, "h3")
                last_values(s)
                turn(s, "h2")
                values(s, 0)
                attend(s, "h1")
                row(s, "last")
                turn(s, "merge")
                attend(s, "h2")
                values(s, 2)
                values(s, 4)
                turn(s, "h3")
                values(s, 1)
                attend(s, "merge")
                turn(s, "last")
                attend(s, "h3")
                values(s, 3)
                values(s, 5)
                attend(s, "last")

            pe.wait_ge(constants_made, CONSTANTS)
            every_step(pe, step)


_INS = ["x", "adj", "L0_gnn_W_heads", "L0_gnn_a_heads", "L0_gnn_W_out", "L0_gnn_a_out", "L0_gnn_w1", "L0_gnn_b1",
        "L0_gnn_w2", "L0_gnn_b2", "L0_gnn_ln_gamma", "L0_gnn_ln_beta", "L1_gnn_W", "L1_gnn_a"]


def kernel(**inputs):
    import numpy as np
    import concourse.bacc as bacc
    from concourse import mybir as mb
    from concourse.bass_utils import run_bass_kernel_spmd

    nc = bacc.Bacc("TRN2", target_bir_lowering=False, num_devices=1)
    arrays, args = {}, []
    for name in _INS:
        a = np.ascontiguousarray(inputs[name])
        arrays[f"in_{name}"] = a
        args.append(nc.dram_tensor(f"in_{name}", a.shape, mb.dt.from_np(a.dtype), kind="ExternalInput").ap())
    shape = arrays["in_x"].shape
    args.append(nc.dram_tensor("out_0", shape, mb.dt.float32, kind="ExternalOutput").ap())
    build_gat(nc, *args)
    r = run_bass_kernel_spmd(nc, [arrays], core_ids=[0])
    return r.results[0]["out_0"]
```

```python
from contextlib import ExitStack

import concourse.bass as bass
from concourse import mybir

F32 = mybir.dt.float32
F32R = mybir.dt.float32r
I32 = mybir.dt.int32
ALU = mybir.AluOpType
ACT = mybir.ActivationFunctionType

P = 128
NORM, VALUES, HEADS, MERGE, FFN, LAST = range(6)
STAGES = 6
CONSTANTS = 3
FOLDS_BEFORE = (0, 5, 8, 11, 13, 14, 16)
LN_EPS = 1e-5
BIG = 1e30
NEG = 1e9


class Unit:

    def __init__(self, name, stage, head, slope):
        self.name, self.stage, self.head, self.slope = name, stage, head, slope


def build_gat(nc, x, adj, W_heads, a_heads, W_out, a_out, w1, b1, w2, b2, gamma, beta, W_last, a_last, out):
    NB, N, D = x.shape
    H = W_heads.shape[0]
    O1 = W_last.shape[1]
    M = N // P
    K = D // P
    KH = H * D // P
    F = 2 * H
    CHUNKS = 3
    VW = (F + H * D) // CHUNKS
    assert N == D == 2 * P and H == 4 and O1 == P and W_heads.shape[2] == D

    UNITS = {u.name: u for u in (
        Unit("h0", HEADS, 0, 0.01), Unit("h1", HEADS, 1, 0.01), Unit("h2", HEADS, 2, 0.01),
        Unit("h3", HEADS, 3, 0.01), Unit("merge", MERGE, 0, 0.01), Unit("last", LAST, 0, 0.2))}
    NAMES = list(UNITS)
    ROWS = ("h2", "h1", "h0", "merge", "h3", "last")
    TURNS = ("h1", "h2", "merge", "h0", "h3", "last")
    ATTENDS = ("h1", "h2", "merge", "h0", "h3", "last")
    PRODUCTS = ("up", "hT", "wo0", "h1T", "wo1", "last1", "last0", "y", "val4", "val3", "val5", "val0", "val1", "val2")
    ELUS = [n for n in NAMES if n != "last"]

    with ExitStack() as ctx:
        def sb(name, shape, dt=F32):
            return ctx.enter_context(nc.sbuf_tensor(name, shape, dt))

        def sem(name):
            return ctx.enter_context(nc.semaphore(name))

        def per_unit(name, names=NAMES):
            return {n: sem(f"{name}_{n}") for n in names}

        ps = ctx.enter_context(nc.psum_tensor("ps", [P, 8, 512], F32))
        bank_row = ps[:, 0, :]
        bank_turn = {n: ps[:, 1 + i % 2, :] for i, n in enumerate(TURNS)}
        bank_att = {n: ps[:, 3 + i % 2, :] for i, n in enumerate(ATTENDS)}
        bank_mm = [ps[:, 5, :], ps[:, 6, :], ps[:, 7, :]]

        Wv = [sb(f"Wv_{s}", [P, K, F + H * D], F32R) for s in ("hi", "lo")]
        Wo = [sb(f"Wo_{s}", [P, KH, D + 2], F32R) for s in ("hi", "lo")]
        Wu = [sb(f"Wu_{s}", [P, K, D], F32R) for s in ("hi", "lo")]
        Wd = [sb(f"Wd_{s}", [P, K, D], F32R) for s in ("hi", "lo")]
        LW = O1 + 2
        Wl_both = sb("Wl", [P, K, 2 * LW], F32R)
        Wl = [Wl_both[:, :, s * LW:(s + 1) * LW] for s in range(2)]
        fold = sb("fold", [P, 2 * H * K + 2 * KH + 2 * K])
        a_rows = sb("a_rows", [P, 2 * H * D + 2 * D + 2 * O1])
        b1_col = sb("b1_col", [P, K])
        b2_col = sb("b2_col", [P, K])
        gamma_rows = sb("gamma_rows", [P, 1, D])
        beta_rows = sb("beta_rows", [P, 1, D])
        ident = sb("ident", [P, P])
        table_in = sb("table_in", [P, M])
        half_neg = sb("half_neg", [P, M])
        adj_sb = sb("adj_sb", [P, M, N], I32)
        mask_first = sb("mask_first", [P, M, N])
        mask_last = sb("mask_last", [P, M, N])

        x_in = [sb(f"x_in{i}", [P, M, D]) for i in range(2)]
        x_res = [sb(f"x_res{i}", [P, M, D]) for i in range(2)]
        xn = [sb(f"xn{i}", [P, M, D]) for i in range(2)]
        hT = [sb(f"hT_{s}", [P, K, N], F32R) for s in ("hi", "lo")]
        fcol_heads = [sb(f"fcol_heads{i}", [P, M, 2 * H]) for i in range(2)]
        last_small = sb("last_small", [P, M, LW])
        last_sum = sb("last_sum", [P, M, LW])
        fcol_one = {"merge": sb("fcol_merge", [P, M, 2]), "last": last_sum[:, :, O1:O1 + 2]}
        val = [[sb(f"val{i}_{s}", [P, M, F + H * D], F32R) for s in ("hi", "lo")] for i in range(2)]
        cat = [sb(f"cat_{s}", [P, KH, N], F32R) for s in ("hi", "lo")]
        val_merge = [sb(f"val_merge_{s}", [P, M, D], F32R) for s in ("hi", "lo")]
        gatT = [[sb(f"gatT{i}_{s}", [P, K, N], F32R) for s in ("hi", "lo")] for i in range(2)]
        ff = sb("ff", [P, K, N])
        ffT = [sb(f"ffT_{s}", [P, K, N], F32R) for s in ("hi", "lo")]
        y_centred = sb("y_centred", [P, M, D])
        x1 = [sb(f"x1_{i}", [P, M, D]) for i in range(2)]
        x1n = [sb(f"x1n{i}", [P, M, D]) for i in range(2)]
        h1T = [sb(f"h1T_{s}", [P, K, N], F32R) for s in ("hi", "lo")]
        val_last_both = sb("val_last", [P, M, 2 * O1], F32R)
        val_last = [val_last_both[:, :, s * O1:(s + 1) * O1] for s in range(2)]
        result = [sb(f"result{i}", [P, M, D]) for i in range(2)]
        LNS = {"x": NORM, "y": FFN, "x1": FFN}
        ln_stats = {n: sb(f"stats_{n}", [P, M, 6]) for n in LNS}
        moments = {n: sb(f"moments_{n}", [P, M, 2]) for n in LNS}
        var_eps = {n: sb(f"var_eps_{n}", [P, M]) for n in LNS}
        mean_neg = {n: sb(f"mean_neg_{n}", [P, M]) for n in LNS}
        rstd = {n: sb(f"rstd_{n}", [P, M]) for n in LNS}

        work = sb("work", [P, len(NAMES) + len(ELUS), M * N])
        probs = {n: work[:, i, :].rearrange("p (m n) -> p m n", m=M) for i, n in enumerate(NAMES)}
        elu = {n: work[:, len(NAMES) + i, :] for i, n in enumerate(ELUS)}
        probsT_two = [[sb(f"probsT{i}_{s}", [P, M, N], F32R) for s in ("hi", "lo")] for i in range(2)]
        probsT = {n: probsT_two[i % 2] for i, n in enumerate(TURNS)}
        row_min = {n: sb(f"row_min_{n}", [P, M]) for n in NAMES}
        row_sum = {n: sb(f"row_sum_{n}", [P, M]) for n in NAMES}
        row_rec = {n: sb(f"row_rec_{n}", [P, M]) for n in NAMES}

        row_made = per_unit("row_made")
        scored = per_unit("scored")
        leaked = per_unit("leaked")
        masked = per_unit("masked")
        exped = per_unit("exped")
        inverted = per_unit("inverted")
        scaled = per_unit("scaled", ELUS)
        turned = per_unit("turned")
        turned_hi = per_unit("turned_hi")
        turned_lo = per_unit("turned_lo")
        attended = per_unit("attended")
        elu_exp = per_unit("elu_exp", ELUS)
        elu_clip = per_unit("elu_clip", ELUS)
        elu_done = per_unit("elu_done", ELUS)
        elu_hi = per_unit("elu_hi", ELUS)
        elu_lo = per_unit("elu_lo", ELUS)
        ln_chain = {n: sem(f"ln_chain_{n}") for n in LNS}
        ln_rstd = {n: sem(f"ln_rstd_{n}") for n in LNS}
        x_loaded = [sem(f"x_loaded{i}") for i in range(2)]
        xn_done = sem("xn_done")
        hT_turned, hT_hi, hT_lo = sem("hT_turned"), sem("hT_hi"), sem("hT_lo")
        fcol_kept = sem("fcol_kept")
        val_made, val_hi, val_lo = sem("val_made"), sem("val_hi"), sem("val_lo")
        wo_made, wo_hi, wo_lo = sem("wo_made"), sem("wo_hi"), sem("wo_lo")
        up_made, up_relu, up_hi, up_lo = sem("up_made"), sem("up_relu"), sem("up_hi"), sem("up_lo")
        b2_added, y_made, y_mean_off, y_gamma = sem("b2_added"), sem("y_made"), sem("y_mean_off"), sem("y_gamma")
        x1_done, x1n_done = sem("x1_done"), sem("x1n_done")
        res_loaded = [sem(f"res_loaded{i}") for i in range(2)]
        res_beta = sem("res_beta")
        h1T_turned, h1T_hi, h1T_lo = sem("h1T_turned"), sem("h1T_hi"), sem("h1T_lo")
        last_made, last_small_kept, last_summed = sem("last_made"), sem("last_small_kept"), sem("last_summed")
        last_hi, last_lo = sem("last_hi"), sem("last_lo")
        result_left, result_right = sem("result_left"), sem("result_right")
        stored = [sem(f"stored{i}") for i in range(2)]
        loaded_heads = [sem(f"loaded_heads{k}") for k in range(K)]
        loaded_a = [sem(f"loaded_a{k}") for k in range(K)]
        loaded_adj, loaded_out, loaded_ffn, loaded_last = sem("loaded_adj"), sem("loaded_out"), sem("loaded_ffn"), sem("loaded_last")
        constants_made = sem("constants_made")
        heads_hi, heads_lo = sem("heads_hi"), sem("heads_lo")
        late_hi, out_split, ffn_split, last_split = sem("late_hi"), sem("out_split"), sem("ffn_split"), sem("last_split")
        set_up_dve = sem("set_up_dve")
        heads_folded, out_folded, last_folded = sem("heads_folded"), sem("out_folded"), sem("last_folded")

        class Step:

            def __init__(self, eng, t=None, pair=None, odd=0, kept=None):
                self.eng, self.t, self.pair, self.odd, self.kept = eng, t, pair, odd, kept

            def runs(self, stage):
                return self.t is None or 0 <= self.t - stage < NB

            def parity(self, stage):
                return (self.odd - stage) % 2 if self.t is None else (self.t - stage) % 2

            def graph(self, stage):
                return 2 * self.pair + (self.odd - stage) if self.t is None else self.t - stage

            def linear(self, slope, offset):
                if (slope, offset) not in self.kept:
                    self.kept[slope, offset] = self.eng.snap(slope * self.pair + offset)
                return self.kept[slope, offset]

            def after(self, semaphore, stage, back=0, per=1, i=None):
                i = per if i is None else i
                if self.t is None:
                    return semaphore, self.linear(2 * per, per * (self.odd - stage - back) + i)
                b = self.t - stage - back
                if b < 0:
                    return constants_made, CONSTANTS
                return semaphore, per * b + i if b < NB else per * NB

            def after_dma(self, pair_of, stage, back=0):
                if self.t is None:
                    b = self.odd - stage - back
                    return pair_of[b % 2], self.linear(16, 16 * (b // 2 + 1))
                b = self.t - stage - back
                if b < 0:
                    return constants_made, CONSTANTS
                return pair_of[b % 2], 16 * (min(b, NB - 2 + b % 2) // 2 + 1)

            def freed(self, order, use):
                at = [o[0] for o in order].index(use)
                for n in range(1, STAGES * len(order)):
                    back, before = divmod(at - n, len(order))
                    _, stage, semaphore, per, i = order[before]
                    if self.t is None or 0 <= self.t - stage + back < NB:
                        return self.after(semaphore, stage, -back, per, i)
                return constants_made, CONSTANTS

        row_order = [(n, UNITS[n].stage, scored[n], 1, 1) for n in ROWS]
        turn_order = {n: [(w, UNITS[w].stage, turned_lo[w], 1, 1) for w in TURNS[i % 2::2]] for i, n in enumerate(TURNS)}
        probsT_order = {n: [(w, UNITS[w].stage, attended[w], 1, 1) for w in TURNS[i % 2::2]] for i, n in enumerate(TURNS)}
        att_order = {n: [(w, UNITS[w].stage, elu_done[w], 1, 1) if w in ELUS else (w, LAST, result_left, 2, 2)
                         for w in ATTENDS[i % 2::2]] for i, n in enumerate(ATTENDS)}
        ATTENDED_LAST = [n for n in ATTENDS if n in ("h0", "h1", "h2", "h3")][-1]
        SCORED_LAST = [n for n in ROWS if n in ("h0", "h1", "h2", "h3")][-1]
        VALS, MERGES, LASTS = [[int(n[-1]) for n in PRODUCTS if n.startswith(k)] for k in ("val", "wo", "last")]
        freed_by = {
            "h1T": (LAST, h1T_lo, 1, 1), "hT": (VALUES, hT_lo, 1, 1),
            **{f"last{m}": (LAST, last_summed, M, LASTS.index(m) + 1) for m in range(M)},
            "up": (FFN, up_relu, 1, 1), "y": (FFN, y_mean_off, 1, 1),
            **{f"val{q}": (VALUES, val_lo, CHUNKS * M, VALS.index(q) + 1) for q in range(CHUNKS * M)},
            **{f"wo{m}": (MERGE, wo_lo, 4, 2 * MERGES.index(m) + 2) for m in range(M)}}
        mm_uses = [(n, *freed_by[n]) for n in PRODUCTS]
        mm_at = {u[0]: i % 3 for i, u in enumerate(mm_uses)}
        mm_order = [mm_uses[i::3] for i in range(3)]

        def bank(use):
            return bank_mm[mm_at[use]]

        STEPS = NB + STAGES - 1
        FIRST = STAGES + STAGES % 2
        LASTP = NB // 2

        def every_step(eng, body, set_up={}):
            for t in range(FIRST):
                if t in set_up:
                    set_up[t]()
                body(Step(eng, t=t))
            with eng.Fori(FIRST // 2, LASTP) as pair:
                kept = {}
                for odd in range(2):
                    body(Step(eng, pair=pair, odd=odd, kept=kept))
            for t in range(2 * LASTP, STEPS):
                body(Step(eng, t=t))

        F_OUT = 2 * H * K
        F_LAST = F_OUT + 2 * KH
        A_OUT = 2 * H * D
        A_LAST = A_OUT + 2 * D

        raw_heads = [work[:, 2 * k:2 * (k + 1), :].rearrange("p a b -> p (a b)") for k in range(K)]
        raw_out = [work[:, NAMES.index("merge"), :], work[:, NAMES.index("last"), :],
                   elu["merge"], x1[0][:].rearrange("p m d -> p (m d)")]
        raw_up, raw_down, raw_last = (t[:].rearrange("p m d -> p (m d)") for t in (x1[1], x1n[0], x1n[1]))
        PER = KH // len(raw_out)

        def elu_from(n):
            return elu[n].rearrange("p (k n) -> p k n", k=K)

        def elu_to(s, n):
            if n == "merge":
                return [t[:] for t in gatT[s.parity(MERGE)]]
            return [t[:, K * UNITS[n].head:K * (UNITS[n].head + 1), :] for t in cat]

        def graph_rows(tensor, s, stage):
            return tensor.rearrange("b (p m) f -> b p m f", m=M)[s.graph(stage)]

        block = ctx.enter_context(nc.Block())

        @block.sync
        def _(sp):
            def load(dst, src, done):
                sp.dma_start(dst, src).then_inc(done, 16)

            def repeated(vector, width, partitions=P):
                return vector.to_broadcast([partitions, width])

            load(x_in[0][:], x.rearrange("b (p m) f -> b p m f", m=M)[0], x_loaded[0])
            heads = W_heads.rearrange("h (k p) o -> k p h o", p=P)
            a_of_heads = a_heads.rearrange("(a h) d -> a (h d)", a=1)
            for k in range(K):
                load(raw_heads[k].rearrange("p (h o) -> p h o", h=H), heads[k], loaded_heads[k])
                part = slice(k * A_OUT // K, (k + 1) * A_OUT // K)
                load(a_rows[:, part], repeated(a_of_heads[:, part], A_OUT // K), loaded_a[k])
            load(x_in[1][:], x.rearrange("b (p m) f -> b p m f", m=M)[1], x_loaded[1])
            load(adj_sb[:], adj.rearrange("(p m) n -> p m n", m=M), loaded_adj)
            for i, dst in enumerate(raw_out):
                load(dst.rearrange("p (k o) -> p k o", k=PER),
                     W_out.rearrange("(i k p) o -> i p k o", p=P, k=PER)[i], loaded_out)
            load(a_rows[:, A_OUT:A_LAST], repeated(a_out.rearrange("(a d) -> a d", a=1), 2 * D), loaded_out)
            for dst, w in ((raw_up, w1), (raw_down, w2)):
                load(dst.rearrange("p (k o) -> p k o", k=K), w.rearrange("(k p) o -> p k o", p=P), loaded_ffn)
            load(gamma_rows[:, 0, :], repeated(gamma.rearrange("(a d) -> a d", a=1), D), loaded_ffn)
            load(beta_rows[:, 0, :], repeated(beta.rearrange("(a d) -> a d", a=1), D), loaded_ffn)
            with nc.allow_non_contiguous_dma(reason="256 values, once"):
                load(b1_col[:], b1.rearrange("(k p) -> p k", p=P), loaded_ffn)
                load(b2_col[:], b2.rearrange("(k p) -> p k", p=P), loaded_ffn)
            load(raw_last[:, 0:K * O1].rearrange("p (k o) -> p k o", k=K),
                 W_last.rearrange("(k p) o -> p k o", p=P), loaded_last)
            load(a_rows[:, A_LAST:], repeated(a_last.rearrange("s o (a) -> a (s o)", a=1), 2 * O1), loaded_last)

            def step(s):
                if s.runs(FFN - 1):
                    sp.wait_ge(*s.after(x1_done, FFN - 1, back=2))
                    par = s.parity(FFN - 1)
                    sp.dma_start(x_res[par][:], graph_rows(x, s, FFN - 1)).then_inc(res_loaded[par], 16)
                if s.t is None or s.t + 2 < NB:
                    sp.wait_ge(*s.after(xn_done, NORM))
                    par = s.parity(NORM)
                    sp.dma_start(x_in[par][:], graph_rows(x, s, NORM - 2)).then_inc(x_loaded[par], 16)
                if s.runs(LAST):
                    sp.wait_ge(*s.after(result_left, LAST, per=2))
                    sp.wait_ge(*s.after(result_right, LAST))
                    par = s.parity(LAST)
                    sp.dma_start(graph_rows(out, s, LAST), result[par][:]).then_inc(stored[par], 16)

            for t in range(FIRST):
                step(Step(sp, t=t))
            with sp.Fori(FIRST // 2, LASTP - 1) as pair:
                kept = {}
                for odd in range(2):
                    step(Step(sp, pair=pair, odd=odd, kept=kept))
            for t in range(2 * LASTP - 2, STEPS):
                step(Step(sp, t=t))
            for par in range(2):
                sp.wait_ge(stored[par], 16 * (NB // 2))

        @block.gpsimd
        def _(pool):
            nc.gpsimd.memset(ident[:], 0.0).then_inc(constants_made, 1)
            nc.gpsimd.memset(half_neg[:], -0.5).then_inc(constants_made, 1)
            pool.wait_ge(constants_made, 2)
            nc.gpsimd.affine_select(out=ident[:], in_=ident[:], compare_op=ALU.not_equal, fill=1.0, base=0,
                                    pattern=[[-1, P]], channel_multiplier=1).then_inc(constants_made, 1)

            def low_part(src, pair, finished):
                nc.gpsimd.tensor_tensor(pair[1], src, pair[0].bitcast(F32), ALU.subtract).then_inc(finished, 1)

            def split_heads():
                for k in range(K):
                    pool.wait_ge(heads_hi, k + 1)
                    low_part(raw_heads[k], [w[:, k, F:] for w in Wv], heads_lo)

            def split_late():
                for i, src in enumerate(raw_out):
                    pool.wait_ge(late_hi, i + 1)
                    low_part(src.rearrange("p (k o) -> p k o", k=PER), [w[:, PER * i:PER * (i + 1), 0:D] for w in Wo], out_split)
                late = len(raw_out)
                for i, (src, pair) in enumerate(((raw_up, Wu), (raw_down, Wd))):
                    pool.wait_ge(late_hi, late + i + 1)
                    low_part(src.rearrange("p (k o) -> p k o", k=K), [w[:] for w in pair], ffn_split)
                pool.wait_ge(late_hi, late + 3)
                low_part(raw_last[:, 0:K * O1].rearrange("p (k o) -> p k o", k=K), [w[:, :, 0:O1] for w in Wl], last_split)

            def rsqrt(s, n):
                if not s.runs(LNS[n]):
                    return
                pool.wait_ge(*s.after(ln_chain[n], LNS[n], per=3))
                nc.gpsimd.tensor_tensor(rstd[n][:], var_eps[n][:], half_neg[:], ALU.pow).then_inc(ln_rstd[n], 1)

            def normalise(s, n, src, dst, done):
                pool.wait_ge(*s.after(ln_rstd[n], LNS[n]))
                pool.nop(nofuse=True)
                for m in range(M):
                    last = nc.gpsimd.tensor_scalar(dst[:, m, :], src[:, m, :], mean_neg[n][:, m:m + 1],
                                                   rstd[n][:, m:m + 1], ALU.add, ALU.mult)
                last.then_inc(done, 1)

            def norm_x(s):
                if not s.runs(NORM):
                    return
                pool.wait_ge(*s.after(hT_turned, NORM, back=2))
                normalise(s, "x", x_in[s.parity(NORM)], xn[s.parity(NORM)], xn_done)

            def norm_x1(s):
                if not s.runs(FFN):
                    return
                pool.wait_ge(*s.after(h1T_turned, FFN, back=2))
                normalise(s, "x1", x1[s.parity(FFN)], x1n[s.parity(FFN)], x1n_done)

            def scale_y(s):
                if not s.runs(FFN):
                    return
                pool.wait_ge(*s.after(y_mean_off, FFN))
                if s.t == FFN:
                    pool.wait_ge(loaded_ffn, 16 * 6)
                nc.gpsimd.tensor_tensor(y_centred[:], y_centred[:], gamma_rows[:].to_broadcast([P, M, D]),
                                        ALU.mult).then_inc(y_gamma, 1)

            def residual(s):
                if not s.runs(FFN):
                    return
                pool.wait_ge(*s.after_dma(res_loaded, FFN))
                if s.t == FFN:
                    pool.wait_ge(loaded_ffn, 16 * 6)
                par = s.parity(FFN)
                nc.gpsimd.tensor_tensor(x_res[par][:], x_res[par][:], beta_rows[:].to_broadcast([P, M, D]),
                                        ALU.add).then_inc(res_beta, 1)

            def second_half(s):
                if not s.runs(LAST):
                    return
                par = s.parity(LAST)
                pool.wait_ge(*s.after(last_summed, LAST, per=M))
                pool.wait_ge(*s.after(x1_done, LAST))
                pool.wait_ge(*s.after_dma(stored, LAST, back=2))
                nc.gpsimd.tensor_tensor(result[par][:, :, O1:D], last_sum[:, :, 0:O1], x1[par][:, :, O1:D],
                                        ALU.add).then_inc(result_right, 1)

            def ffn_hi(s):
                if not s.runs(FFN):
                    return
                pool.wait_ge(*s.after(up_relu, FFN))
                pool.wait_ge(*s.after(y_made, FFN, back=1))
                pool.nop(nofuse=True)
                nc.gpsimd.tensor_scalar(ffT[0][:], ff[:], 1.0, 0.0, ALU.mult, ALU.add).then_inc(up_hi, 1)

            def ffn_lo(s):
                if not s.runs(FFN):
                    return
                pool.wait_ge(*s.after(up_hi, FFN))
                nc.gpsimd.tensor_tensor(ffT[1][:], ff[:], ffT[0][:].bitcast(F32), ALU.subtract).then_inc(up_lo, 1)

            def scale(s, n):
                u = UNITS[n]
                if not s.runs(u.stage):
                    return
                pool.wait_ge(*s.after(inverted[n], u.stage))
                pool.nop(nofuse=True)
                for m in range(M):
                    last = nc.gpsimd.tensor_scalar(probs[n][:, m, :], probs[n][:, m, :], row_rec[n][:, m:m + 1],
                                                   1.0, ALU.mult, ALU.mult)
                last.then_inc(scaled[n], 1)

            def split_hi(s, n):
                u = UNITS[n]
                if not s.runs(u.stage):
                    return
                pool.wait_ge(*s.after(elu_done[n], u.stage))
                if n == "merge":
                    pool.wait_ge(*s.after(up_made, MERGE, back=2))
                    pool.nop(nofuse=True)
                else:
                    pool.wait_ge(*s.after(wo_made, HEADS, back=1, per=2))
                    pool.nop(nofuse=True)
                nc.gpsimd.tensor_scalar(elu_to(s, n)[0], elu_from(n), 1.0, 0.0, ALU.mult, ALU.add).then_inc(elu_hi[n], 1)

            def split_lo(s, n):
                u = UNITS[n]
                if not s.runs(u.stage):
                    return
                hi, lo = elu_to(s, n)
                pool.wait_ge(*s.after(elu_hi[n], u.stage))
                nc.gpsimd.tensor_tensor(lo, elu_from(n), hi.bitcast(F32), ALU.subtract).then_inc(elu_lo[n], 1)

            def step(s):
                residual(s)
                ffn_hi(s)
                scale(s, "h1")
                ffn_lo(s)
                scale(s, "h2")
                rsqrt(s, "x")
                scale(s, "merge")
                rsqrt(s, "y")
                scale(s, "h0")
                scale_y(s)
                norm_x(s)
                split_hi(s, "h1")
                scale(s, "h3")
                second_half(s)
                split_hi(s, "h2")
                split_lo(s, "h2")
                split_lo(s, "h1")
                split_hi(s, "merge")
                split_lo(s, "merge")
                split_hi(s, "h0")
                split_hi(s, "h3")
                rsqrt(s, "x1")
                norm_x1(s)

            pool.wait_ge(constants_made, CONSTANTS)
            every_step(pool, step, {1: split_heads, 2: split_late})

        @block.scalar
        def _(act):
            def hi_copy(dst, src, done, func=ACT.Identity):
                nc.scalar.activation(dst, src, func).then_inc(done, 1)

            def scores(s, n):
                u = UNITS[n]
                if not s.runs(u.stage):
                    return
                act.wait_ge(*s.after(row_made[n], u.stage))
                act.wait_ge(*s.after(turned[n], u.stage, back=1))
                col = fcol_heads[s.parity(HEADS)] if u.stage == HEADS else fcol_one[n]
                for m in range(M):
                    last = nc.scalar.activation(probs[n][:, m, :], bank_row[:, 0:N], ACT.Identity,
                                                bias=col[:, m, u.head:u.head + 1])
                last.then_inc(scored[n], 1)

            def exps(s, n):
                u = UNITS[n]
                if not s.runs(u.stage):
                    return
                act.wait_ge(*s.after(masked[n], u.stage))
                for m in range(M):
                    last = nc.scalar.activation(probs[n][:, m, :], probs[n][:, m, :], ACT.Exp, scale=-1.0,
                                                bias=row_min[n][:, m:m + 1], accum_out=row_sum[n][:, m:m + 1])
                last.then_inc(exped[n], 1)

            def turn_hi(s, n):
                u = UNITS[n]
                if not s.runs(u.stage):
                    return
                act.wait_ge(*s.after(turned[n], u.stage))
                act.wait_ge(*s.freed(probsT_order[n], n))
                hi_copy(probsT[n][0][:].rearrange("p m n -> p (m n)"), bank_turn[n], turned_hi[n])

            def elu_exps(s, n):
                u = UNITS[n]
                if not s.runs(u.stage):
                    return
                act.wait_ge(*s.after(attended[n], u.stage))
                act.wait_ge(*s.after(elu_lo[n], u.stage, back=1))
                if n == "merge":
                    act.wait_ge(*s.after(y_made, MERGE, back=1))
                nc.scalar.activation(elu[n], bank_att[n], ACT.Exp).then_inc(elu_exp[n], 1)

            def clip(s, n):
                u = UNITS[n]
                if not s.runs(u.stage):
                    return
                act.wait_ge(*s.after(elu_exp[n], u.stage))
                nc.scalar.activation(elu[n], elu[n], ACT.Relu, bias=1.0, scale=-1.0).then_inc(elu_clip[n], 1)

            def turn_x(s):
                if not s.runs(VALUES):
                    return
                act.wait_ge(*s.after(hT_turned, VALUES))
                act.wait_ge(*s.after(val_made, VALUES, back=1, per=CHUNKS * M))
                hi_copy(hT[0][:].rearrange("p k n -> p (k n)"), bank("hT"), hT_hi, ACT.Relu)

            def value_hi(s, q):
                if not s.runs(VALUES):
                    return
                m, c = divmod(q, CHUNKS)
                act.wait_ge(*s.after(val_made, VALUES, per=CHUNKS * M, i=VALS.index(q) + 1))
                act.wait_ge(*s.after(attended[ATTENDED_LAST], HEADS + 1))
                hi_copy(val[s.parity(VALUES)][0][:, m, c * VW:(c + 1) * VW], bank(f"val{q}")[:, 0:VW], val_hi)
                if s.t == VALUES:
                    high_late(VALS.index(q))

            def merge_hi(s, m):
                if not s.runs(MERGE):
                    return
                act.wait_ge(*s.after(wo_made, MERGE, per=2, i=MERGES.index(m) + 1))
                act.wait_ge(*s.after(attended["merge"], MERGE, back=1))
                hi_copy(val_merge[0][:, m, :], bank(f"wo{m}")[:, 0:D], wo_hi)

            def add_b2(s):
                if not s.runs(FFN):
                    return
                act.wait_ge(*s.after(elu_hi["merge"], FFN))
                act.wait_ge(*s.after(elu_lo["merge"], FFN))
                for k in range(K):
                    at = elu_from("merge")[:, k, :]
                    last = nc.scalar.activation(at, at, ACT.Identity, bias=b2_col[:, k:k + 1])
                last.then_inc(b2_added, 1)

            def centre_y(s):
                if not s.runs(FFN):
                    return
                act.wait_ge(*s.after(ln_chain["y"], FFN, per=3))
                act.wait_ge(*s.after(x1_done, FFN, back=1))
                for m in range(M):
                    last = nc.scalar.activation(y_centred[:, m, :], bank("y")[:, m * D:(m + 1) * D], ACT.Identity,
                                                bias=mean_neg["y"][:, m:m + 1])
                last.then_inc(y_mean_off, 1)

            def ffn_relu(s):
                if not s.runs(FFN):
                    return
                act.wait_ge(*s.after(up_made, FFN))
                act.wait_ge(*s.after(up_lo, FFN, back=1))
                for k in range(K):
                    last = nc.scalar.activation(ff[:, k, :], bank("up")[:, k * N:(k + 1) * N], ACT.Relu,
                                                bias=b1_col[:, k:k + 1])
                last.then_inc(up_relu, 1)

            def turn_x1(s):
                if not s.runs(LAST):
                    return
                act.wait_ge(*s.after(h1T_turned, LAST))
                act.wait_ge(*s.after(last_made, LAST, back=1, per=M))
                hi_copy(h1T[0][:].rearrange("p k n -> p (k n)"), bank("h1T"), h1T_hi, ACT.Relu)

            def last_small_part(s, m):
                if not s.runs(LAST):
                    return
                i = LASTS.index(m) + 1
                act.wait_ge(*s.after(last_made, LAST, per=M, i=i))
                act.wait_ge(*s.after(last_summed, LAST, back=1, per=M))
                nc.scalar.activation(last_small[:, m, :], bank(f"last{m}")[:, LW:2 * LW], ACT.Identity).then_inc(last_small_kept, 1)

            def last_hi_copy(s):
                if not s.runs(LAST):
                    return
                act.wait_ge(*s.after(last_summed, LAST, per=M))
                act.wait_ge(*s.after(attended["last"], LAST, back=1))
                hi_copy(val_last[0], last_sum[:, :, 0:O1], last_hi)

            def step(s):
                scores(s, "h2")
                scores(s, "h1")
                turn_x(s)
                add_b2(s)
                ffn_relu(s)
                merge_hi(s, 0)
                exps(s, "h1")
                turn_x1(s)
                scores(s, "h0")
                exps(s, "h2")
                merge_hi(s, 1)
                last_small_part(s, 1)
                turn_hi(s, "h1")
                scores(s, "merge")
                last_small_part(s, 0)
                exps(s, "h0")
                scores(s, "h3")
                exps(s, "merge")
                turn_hi(s, "h2")
                scores(s, "last")
                value_hi(s, 4)
                centre_y(s)
                elu_exps(s, "h1")
                turn_hi(s, "merge")
                clip(s, "h1")
                exps(s, "h3")
                elu_exps(s, "h2")
                turn_hi(s, "h0")
                clip(s, "h2")
                exps(s, "last")
                value_hi(s, 3)
                elu_exps(s, "merge")
                turn_hi(s, "h3")
                clip(s, "merge")
                value_hi(s, 5)
                elu_exps(s, "h0")
                last_hi_copy(s)
                clip(s, "h0")
                turn_hi(s, "last")
                value_hi(s, 0)
                value_hi(s, 1)
                elu_exps(s, "h3")
                clip(s, "h3")
                value_hi(s, 2)

            def high_heads():
                for k in range(K):
                    act.wait_ge(loaded_heads[k], 16)
                    hi_copy(Wv[0][:, k, F:], raw_heads[k], heads_hi)

            def high_late(i):
                late = len(raw_out)
                if i == 0:
                    act.wait_ge(loaded_out, 16 * (late + 1))
                if i < late:
                    hi_copy(Wo[0][:, PER * i:PER * (i + 1), 0:D], raw_out[i].rearrange("p (k o) -> p k o", k=PER), late_hi)
                if i == late:
                    act.wait_ge(loaded_ffn, 16 * 6)
                    hi_copy(Wu[0][:], raw_up.rearrange("p (k o) -> p k o", k=K), late_hi)
                if i == late + 1:
                    hi_copy(Wd[0][:], raw_down.rearrange("p (k o) -> p k o", k=K), late_hi)
                    act.wait_ge(loaded_last, 32)
                    hi_copy(Wl[0][:, :, 0:O1], raw_last[:, 0:K * O1].rearrange("p (k o) -> p k o", k=K), late_hi)

            act.wait_ge(constants_made, CONSTANTS)
            nc.scalar.activation(table_in[:], half_neg[:], ACT.Exp)
            every_step(act, step, {1: high_heads})

        @block.vector
        def _(dve):
            done = [0]

            def chained(instruction):
                done[0] += 1
                instruction.then_inc(set_up_dve, 1)

            unused = [t[:, m, :] for t in result for m in range(M)]
            folded = []

            def fold_vector(w, a, dst, width):
                if len(folded) >= len(unused):
                    dve.wait_ge(set_up_dve, folded[-len(unused)])
                chained(nc.vector.tensor_tensor_reduce(unused[len(folded) % len(unused)][:, 0:width], w, a, -1.0, 0.0,
                                                       ALU.mult, ALU.add, dst))
                folded.append(done[0])

            def split_folds(pair, columns, finished):
                hi, lo = pair
                dve.wait_ge(set_up_dve, done[0])
                chained(nc.vector.tensor_copy(hi, columns))
                dve.wait_ge(set_up_dve, done[0])
                nc.vector.tensor_tensor(lo, columns, hi.bitcast(F32), ALU.subtract).then_inc(finished, 1)

            def fold_heads():
                for part in range(K):
                    dve.wait_ge(loaded_a[part], 16)
                    for k in range(K):
                        dve.wait_ge(loaded_heads[k], 16)
                        for h in range(part * H // K, (part + 1) * H // K):
                            for side in range(2):
                                at = 2 * H * k + side * H + h
                                fold_vector(raw_heads[k][:, h * D:(h + 1) * D],
                                            a_rows[:, (2 * h + side) * D:(2 * h + side + 1) * D], fold[:, at:at + 1], D)
                    if part == 0:
                        low_x(Step(dve, t=VALUES))
                split_folds([w[:, :, 0:F] for w in Wv], fold[:, 0:F_OUT].rearrange("p (k f) -> p k f", k=K), heads_folded)

            keys = adj_sb[:].rearrange("p m (q w) -> p m w q", w=M)
            out_vectors = [(k, side) for k in range(KH) for side in range(2)]

            def mask_and_fold_out(i):
                if i == 0:
                    dve.wait_ge(loaded_adj, 16)
                    for m in range(M):
                        chained(nc.vector.tensor_scalar(mask_first[:, m, :].rearrange("p (w q) -> p w q", w=M), keys[:, m],
                                                        0.0, BIG, ALU.is_le, ALU.mult))
                    dve.wait_ge(loaded_out, 16 * (len(raw_out) + 1))
                fold_out(out_vectors[FOLDS_BEFORE[i]:FOLDS_BEFORE[i + 1]])

            def fold_out(vectors):
                for k, side in vectors:
                    j = k % PER
                    fold_vector(raw_out[k // PER][:, j * D:(j + 1) * D], a_rows[:, A_OUT + side * D:A_OUT + (side + 1) * D],
                                fold[:, F_OUT + 2 * k + side:F_OUT + 2 * k + side + 1], D)

            def end_out():
                fold_out(out_vectors[FOLDS_BEFORE[-1]:])
                split_folds([w[:, :, D:D + 2] for w in Wo], fold[:, F_OUT:F_LAST].rearrange("p (k s) -> p k s", s=2), out_folded)

            def make_mask_last():
                for m in range(M):
                    chained(nc.vector.tensor_scalar(mask_last[:, m, :].rearrange("p (w q) -> p w q", w=M), keys[:, m],
                                                    -NEG, NEG, ALU.mult, ALU.add))

            def fold_last():
                dve.wait_ge(loaded_last, 32)
                for k in range(K):
                    for side in range(2):
                        fold_vector(raw_last[:, k * O1:(k + 1) * O1], a_rows[:, A_LAST + side * O1:A_LAST + (side + 1) * O1],
                                    fold[:, F_LAST + 2 * k + side:F_LAST + 2 * k + side + 1], O1)
                split_folds([w[:, :, O1:O1 + 2] for w in Wl], fold[:, F_LAST:].rearrange("p (k s) -> p k s", s=2), last_folded)

            def stats(s, n, src):
                dve.wait_ge(*s.after(ln_rstd[n], LNS[n], back=1))
                dve.wait_ge(*s.after({"x": xn_done, "y": x1_done, "x1": x1n_done}[n], LNS[n], back=1))
                for m in range(M):
                    last = nc.vector.bn_stats(ln_stats[n][:, m, :], src(m))
                last.then_inc(ln_chain[n], 1)

            def aggregate(s, n):
                if not s.runs(LNS[n]):
                    return
                dve.wait_ge(*s.after(ln_chain[n], LNS[n], per=3, i=1))
                dve.nop(nofuse=True)
                for m in range(M):
                    last = nc.vector.bn_aggr(moments[n][:, m, :], ln_stats[n][:, m, :])
                last.then_inc(ln_chain[n], 1)

            def mean_and_var(s, n):
                if not s.runs(LNS[n]):
                    return
                dve.wait_ge(*s.after(ln_chain[n], LNS[n], per=3, i=2))
                nc.vector.tensor_scalar(mean_neg[n][:], moments[n][:, :, 0], -1.0, None, ALU.mult)
                nc.vector.tensor_scalar(var_eps[n][:], moments[n][:, :, 1], LN_EPS, None, ALU.add).then_inc(ln_chain[n], 1)

            def stats_x(s):
                if s.runs(NORM):
                    dve.wait_ge(*s.after_dma(x_loaded, NORM))
                    stats(s, "x", lambda m: x_in[s.parity(NORM)][:, m, :])

            def stats_y(s):
                if s.runs(FFN):
                    dve.wait_ge(*s.after(y_made, FFN))
                    stats(s, "y", lambda m: bank("y")[:, m * D:(m + 1) * D])

            def stats_x1(s):
                if s.runs(FFN):
                    dve.wait_ge(*s.after(x1_done, FFN))
                    stats(s, "x1", lambda m: x1[s.parity(FFN)][:, m, :])

            def leak(s, n):
                u = UNITS[n]
                if not s.runs(u.stage):
                    return
                dve.wait_ge(*s.after(scored[n], u.stage))
                nc.vector.scalar_tensor_tensor(out=probs[n], in0=probs[n], scalar=u.slope, in1=probs[n],
                                               op0=ALU.mult, op1=ALU.min).then_inc(leaked[n], 1)

            def mask_and_min(s, n):
                u = UNITS[n]
                if not s.runs(u.stage):
                    return
                dve.wait_ge(*s.after(leaked[n], u.stage))
                dve.nop(nofuse=True)
                mask = mask_last if n == "last" else mask_first
                for m in range(M):
                    last = nc.vector.tensor_tensor_reduce(probs[n][:, m, :], probs[n][:, m, :], mask[:, m, :],
                                                          1.0, 3e38, ALU.add, ALU.min, row_min[n][:, m:m + 1])
                last.then_inc(masked[n], 1)

            def invert(s, n):
                u = UNITS[n]
                if not s.runs(u.stage):
                    return
                dve.wait_ge(*s.after(exped[n], u.stage))
                nc.vector.reciprocal(row_rec[n][:], row_sum[n][:]).then_inc(inverted[n], 1)

            def turn_lo(s, n):
                u = UNITS[n]
                if not s.runs(u.stage):
                    return
                hi, lo = (t[:].rearrange("p m n -> p (m n)") for t in probsT[n])
                dve.wait_ge(*s.after(turned_hi[n], u.stage))
                nc.vector.tensor_tensor(lo, bank_turn[n], hi.bitcast(F32), ALU.subtract).then_inc(turned_lo[n], 1)

            def elus(s, n):
                u = UNITS[n]
                if not s.runs(u.stage):
                    return
                dve.wait_ge(*s.after(elu_clip[n], u.stage))
                nc.vector.scalar_tensor_tensor(out=elu[n], in0=elu[n], scalar=-1.0, in1=bank_att[n],
                                               op0=ALU.mult, op1=ALU.max).then_inc(elu_done[n], 1)

            def split_lo(s, n):
                u = UNITS[n]
                if not s.runs(u.stage):
                    return
                hi, lo = elu_to(s, n)
                dve.wait_ge(*s.after(elu_hi[n], u.stage))
                nc.vector.tensor_tensor(lo, elu_from(n), hi.bitcast(F32), ALU.subtract).then_inc(elu_lo[n], 1)

            def relu_lo(pair, src, finished):
                hi, lo = (t[:].rearrange("p k n -> p (k n)") for t in pair)
                nc.vector.scalar_tensor_tensor(out=lo, in0=src, scalar=0.0, in1=hi.bitcast(F32),
                                               op0=ALU.max, op1=ALU.subtract).then_inc(finished, 1)

            def turn_x(s):
                if s.runs(VALUES) and s.t != VALUES:
                    low_x(s)

            def low_x(s):
                dve.wait_ge(*s.after(hT_hi, VALUES))
                relu_lo(hT, bank("hT"), hT_lo)

            def value_lo(s, q):
                if not s.runs(VALUES):
                    return
                if s.t == VALUES:
                    mask_and_fold_out(VALS.index(q))
                m, c = divmod(q, CHUNKS)
                hi, lo = (t[:, m, c * VW:(c + 1) * VW] for t in val[s.parity(VALUES)])
                dve.wait_ge(*s.after(val_hi, VALUES, per=CHUNKS * M, i=VALS.index(q) + 1))
                if c == 0:
                    dve.wait_ge(*s.after(scored[SCORED_LAST], HEADS + 1))
                    nc.vector.tensor_copy(fcol_heads[s.parity(VALUES)][:, m, :], bank(f"val{q}")[:, 0:F]).then_inc(fcol_kept, 1)
                nc.vector.tensor_tensor(lo, bank(f"val{q}")[:, 0:VW], hi.bitcast(F32), ALU.subtract).then_inc(val_lo, 1)

            def merge_lo(s, m):
                if not s.runs(MERGE):
                    return
                hi, lo = (t[:, m, :] for t in val_merge)
                dve.wait_ge(*s.after(wo_hi, MERGE, per=2, i=MERGES.index(m) + 1))
                nc.vector.tensor_tensor(lo, bank(f"wo{m}")[:, 0:D], hi.bitcast(F32), ALU.subtract).then_inc(wo_lo, 1)
                dve.wait_ge(*s.after(scored["merge"], MERGE, back=1))
                nc.vector.tensor_copy(fcol_one["merge"][:, m, :], bank(f"wo{m}")[:, D:D + 2]).then_inc(wo_lo, 1)

            def make_x1(s):
                if not s.runs(FFN):
                    return
                par = s.parity(FFN)
                dve.wait_ge(*s.after(y_gamma, FFN))
                dve.wait_ge(*s.after(ln_rstd["y"], FFN))
                dve.wait_ge(*s.after(res_beta, FFN))
                dve.wait_ge(*s.after(result_left, FFN, back=2, per=2))
                dve.wait_ge(*s.after(result_right, FFN, back=2))
                for m in range(M):
                    last = nc.vector.scalar_tensor_tensor(out=x1[par][:, m, :], in0=y_centred[:, m, :],
                                                          scalar=rstd["y"][:, m:m + 1], in1=x_res[par][:, m, :],
                                                          op0=ALU.mult, op1=ALU.add)
                last.then_inc(x1_done, 1)

            def turn_x1(s):
                if s.runs(LAST):
                    dve.wait_ge(*s.after(h1T_hi, LAST))
                    relu_lo(h1T, bank("h1T"), h1T_lo)

            def last_add(s, m):
                if not s.runs(LAST):
                    return
                dve.wait_ge(*s.after(last_small_kept, LAST, per=M, i=LASTS.index(m) + 1))
                dve.wait_ge(*s.after(last_lo, LAST, back=1))
                dve.wait_ge(*s.after(scored["last"], LAST, back=1))
                dve.wait_ge(*s.after(result_right, LAST, back=1))
                nc.vector.tensor_tensor(last_sum[:, m, :], bank(f"last{m}")[:, 0:LW], last_small[:, m, :],
                                        ALU.add).then_inc(last_summed, 1)

            def last_low_part(s):
                if not s.runs(LAST):
                    return
                dve.wait_ge(*s.after(last_hi, LAST))
                nc.vector.tensor_tensor(val_last[1], last_sum[:, :, 0:O1], val_last[0].bitcast(F32),
                                        ALU.subtract).then_inc(last_lo, 1)

            def last_result(s):
                if not s.runs(LAST):
                    return
                par = s.parity(LAST)
                dve.wait_ge(*s.after(attended["last"], LAST))
                dve.wait_ge(*s.after(inverted["last"], LAST))
                dve.wait_ge(*s.after_dma(stored, LAST, back=2))
                for part, added in ((1, x1[par]), (0, result[par])):
                    if part == 0:
                        dve.wait_ge(*s.after(result_left, LAST, per=2, i=1))
                    for m in range(M):
                        o = (2 * m + part) * O1
                        last = nc.vector.scalar_tensor_tensor(out=result[par][:, m, 0:O1], in0=bank_att["last"][:, o:o + O1],
                                                              scalar=row_rec["last"][:, m:m + 1], in1=added[:, m, 0:O1],
                                                              op0=ALU.mult, op1=ALU.add)
                    last.then_inc(result_left, 1)

            def step(s):
                leak(s, "h1")
                turn_x(s)
                mask_and_min(s, "h1")
                leak(s, "h2")
                merge_lo(s, 0)
                mask_and_min(s, "h2")
                invert(s, "h1")
                turn_x1(s)
                stats_x(s)
                leak(s, "h0")
                aggregate(s, "x")
                merge_lo(s, 1)
                invert(s, "h2")
                mask_and_min(s, "h0")
                turn_lo(s, "h1")
                leak(s, "merge")
                last_add(s, 1)
                mask_and_min(s, "merge")
                mean_and_var(s, "x")
                last_add(s, 0)
                stats_y(s)
                invert(s, "h0")
                leak(s, "h3")
                invert(s, "merge")
                aggregate(s, "y")
                mean_and_var(s, "y")
                turn_lo(s, "h2")
                leak(s, "last")
                mask_and_min(s, "h3")
                mask_and_min(s, "last")
                turn_lo(s, "merge")
                elus(s, "h1")
                make_x1(s)
                invert(s, "h3")
                value_lo(s, 4)
                turn_lo(s, "h0")
                elus(s, "h2")
                stats_x1(s)
                value_lo(s, 3)
                aggregate(s, "x1")
                turn_lo(s, "h3")
                elus(s, "merge")
                value_lo(s, 5)
                mean_and_var(s, "x1")
                last_low_part(s)
                elus(s, "h0")
                turn_lo(s, "last")
                invert(s, "last")
                value_lo(s, 0)
                value_lo(s, 1)
                elus(s, "h3")
                split_lo(s, "h0")
                value_lo(s, 2)
                split_lo(s, "h3")
                last_result(s)

            dve.wait_ge(constants_made, CONSTANTS)
            every_step(dve, step, {1: fold_heads, 2: end_out, 3: make_mask_last, 4: fold_last})

        @block.tensor
        def _(pe):
            spare = bank_turn[TURNS[1 - TURNS.index("last") % 2]][:, 0:P]

            def keep_clock(turns):
                for _ in range(turns):
                    nc.tensor.transpose(spare, ident[:], ident[:])

            def last_alone(s):
                return s.t is not None and s.t >= STEPS - 2

            def three(out_ap, lhs, rhs, first, final):
                passes = ((lhs[0], rhs[1]), (lhs[1], rhs[0]), (lhs[0], rhs[0]))
                for i, (l, r) in enumerate(passes):
                    ins = nc.tensor.matmul(out_ap, l, r, start=first and i == 0, stop=final and i == 2)
                return ins

            def row(s, n):
                u = UNITS[n]
                if not s.runs(u.stage):
                    return
                if u.stage == HEADS:
                    pe.wait_ge(*s.after(fcol_kept, HEADS, per=M))
                    col, at = fcol_heads[s.parity(HEADS)], H + u.head
                else:
                    pe.wait_ge(*(s.after(wo_lo, MERGE, per=4) if n == "merge" else s.after(last_summed, LAST, per=M)))
                    col, at = fcol_one[n], 1
                if s.t == HEADS and n in [w for w in ROWS if UNITS[w].stage == HEADS][1:3]:
                    keep_clock(9)
                if n == "last" and s.t == STEPS - 1:
                    keep_clock(8)
                pe.wait_ge(*s.freed(row_order, n))
                for m in range(M):
                    last = nc.tensor.transpose(bank_row[:, m * P:(m + 1) * P],
                                               col[:, m, at:at + 1].to_broadcast([P, P]), ident[:])
                last.then_inc(row_made[n], 1)

            def turn(s, n):
                u = UNITS[n]
                if not s.runs(u.stage):
                    return
                if s.t == HEADS and n == TURNS[0]:
                    keep_clock(21)
                if n == "last" and last_alone(s):
                    keep_clock(26)
                if n == "last":
                    pe.wait_ge(*s.after(exped[n], u.stage))
                else:
                    pe.wait_ge(*s.after(scaled[n], u.stage))
                pe.wait_ge(*s.freed(turn_order[n], n))
                for m in range(M):
                    for j in range(M):
                        last = nc.tensor.transpose(bank_turn[n][:, j * N + m * P:j * N + (m + 1) * P],
                                                   probs[n][:, m, j * P:(j + 1) * P], ident[:])
                last.then_inc(turned[n], 1)

            def attend(s, n):
                u = UNITS[n]
                if not s.runs(u.stage):
                    return
                if n == "last" and last_alone(s):
                    keep_clock(13)
                pe.wait_ge(*s.after(turned_lo[n], u.stage))
                if u.stage == HEADS:
                    pe.wait_ge(*s.after(val_lo, HEADS, per=CHUNKS * M))
                if n == "last":
                    pe.wait_ge(*s.after(last_lo, LAST))
                pe.wait_ge(*s.freed(att_order[n], n))
                to = bank_att[n]
                pT = probsT[n]
                if n == "last":
                    for m in range(M):
                        for j in range(M):
                            p_hi, p_lo = (t[:, j, m * P:(m + 1) * P] for t in pT)
                            nc.tensor.matmul(to[:, 2 * m * O1:2 * (m + 1) * O1], p_hi, val_last_both[:, j, :],
                                             start=j == 0, stop=False)
                            last = nc.tensor.matmul(to[:, 2 * m * O1:(2 * m + 1) * O1], p_lo, val_last[0][:, j, :],
                                                    start=False, stop=j == M - 1)
                else:
                    v = val[s.parity(HEADS)] if u.stage == HEADS else val_merge
                    for k in range(K):
                        c = (F if u.stage == HEADS else 0) + u.head * D + k * P
                        for j in range(M):
                            last = three(to[:, k * N:(k + 1) * N], [t[:, j, c:c + P] for t in v],
                                         [t[:, j, :] for t in pT], j == 0, j == M - 1)
                last.then_inc(attended[n], 1)

            def turn_nodes(use, src, finished):
                for k in range(K):
                    for m in range(M):
                        last = nc.tensor.transpose(bank(use)[:, k * N + m * P:k * N + (m + 1) * P],
                                                   src[:, m, k * P:(k + 1) * P], ident[:])
                last.then_inc(finished, 1)

            def turn_x(s):
                if not s.runs(VALUES):
                    return
                pe.wait_ge(*s.after(xn_done, VALUES))
                pe.wait_ge(*s.freed(mm_order[mm_at["hT"]], "hT"))
                turn_nodes("hT", xn[s.parity(VALUES)], hT_turned)

            def values(s, q):
                if not s.runs(VALUES):
                    return
                m, c = divmod(q, CHUNKS)
                pe.wait_ge(*s.after(hT_lo, VALUES))
                if s.t == VALUES:
                    if q == VALS[0]:
                        keep_clock(24)
                    pe.wait_ge(heads_lo, K)
                    pe.wait_ge(heads_folded, 1)
                pe.wait_ge(*s.freed(mm_order[mm_at[f"val{q}"]], f"val{q}"))
                for k in range(K):
                    last = three(bank(f"val{q}")[:, 0:VW], [t[:, k, m * P:(m + 1) * P] for t in hT],
                                 [w[:, k, c * VW:(c + 1) * VW] for w in Wv], k == 0, k == K - 1)
                last.then_inc(val_made, 1)

            def merge(s, m):
                if not s.runs(MERGE):
                    return
                for n in ("h0", "h1", "h2", "h3"):
                    pe.wait_ge(*s.after(elu_lo[n], MERGE))
                if s.t == MERGE:
                    pe.wait_ge(out_split, len(raw_out))
                    pe.wait_ge(out_folded, 1)
                pe.wait_ge(*s.freed(mm_order[mm_at[f"wo{m}"]], f"wo{m}"))
                for c in range(KH):
                    last = three(bank(f"wo{m}")[:, 0:D + 2], [t[:, c, m * P:(m + 1) * P] for t in cat],
                                 [w[:, c, :] for w in Wo], c == 0, c == KH - 1)
                last.then_inc(wo_made, 1)

            def ffn_up(s):
                if not s.runs(FFN):
                    return
                g = gatT[s.parity(FFN)]
                pe.wait_ge(*s.after(elu_lo["merge"], FFN))
                if s.t == FFN:
                    pe.wait_ge(ffn_split, 2)
                pe.wait_ge(*s.freed(mm_order[mm_at["up"]], "up"))
                for d in range(K):
                    for k in range(K):
                        last = three(bank("up")[:, d * N:(d + 1) * N], [w[:, k, d * P:(d + 1) * P] for w in Wu],
                                     [t[:, k, :] for t in g], k == 0, k == K - 1)
                last.then_inc(up_made, 1)

            def ffn_down(s):
                if not s.runs(FFN):
                    return
                pe.wait_ge(*s.after(up_lo, FFN))
                pe.wait_ge(*s.after(b2_added, FFN))
                pe.wait_ge(*s.freed(mm_order[mm_at["y"]], "y"))
                for m in range(M):
                    nodes = slice(m * P, (m + 1) * P)
                    to = bank("y")[:, m * D:(m + 1) * D]
                    for k in range(K):
                        nc.tensor.matmul(to[:, k * P:(k + 1) * P], elu_from("merge")[:, k, nodes], ident[:],
                                         is_transpose=True, start=k == 0, stop=False)
                    for k in range(K):
                        last = three(to, [t[:, k, nodes] for t in ffT], [w[:, k, :] for w in Wd], False, k == K - 1)
                last.then_inc(y_made, 1)

            def turn_x1(s):
                if not s.runs(LAST):
                    return
                pe.wait_ge(*s.after(x1n_done, LAST))
                pe.wait_ge(*s.freed(mm_order[mm_at["h1T"]], "h1T"))
                turn_nodes("h1T", x1n[s.parity(LAST)], h1T_turned)

            def last_values(s, m):
                if not s.runs(LAST):
                    return
                if last_alone(s) and m == LASTS[0]:
                    keep_clock(12)
                pe.wait_ge(*s.after(h1T_lo, LAST))
                if s.t == LAST:
                    pe.wait_ge(last_split, 1)
                    pe.wait_ge(last_folded, 1)
                pe.wait_ge(*s.freed(mm_order[mm_at[f"last{m}"]], f"last{m}"))
                to = bank(f"last{m}")
                for k in range(K):
                    h_hi, h_lo = (t[:, k, m * P:(m + 1) * P] for t in h1T)
                    nc.tensor.matmul(to[:, 0:2 * LW], h_hi, Wl_both[:, k, :], start=k == 0, stop=False)
                    last = nc.tensor.matmul(to[:, 0:LW], h_lo, Wl[0][:, k, :], start=False, stop=k == K - 1)
                last.then_inc(last_made, 1)

            def step(s):
                row(s, "h2")
                ffn_up(s)
                row(s, "h1")
                turn_x(s)
                merge(s, 0)
                turn_x1(s)
                row(s, "h0")
                merge(s, 1)
                turn(s, "h1")
                last_values(s, 1)
                last_values(s, 0)
                row(s, "merge")
                ffn_down(s)
                row(s, "h3")
                values(s, 4)
                turn(s, "h2")
                row(s, "last")
                attend(s, "h1")
                values(s, 3)
                turn(s, "merge")
                attend(s, "h2")
                turn(s, "h0")
                values(s, 5)
                attend(s, "merge")
                values(s, 0)
                turn(s, "h3")
                attend(s, "h0")
                values(s, 1)
                turn(s, "last")
                attend(s, "h3")
                values(s, 2)
                attend(s, "last")

            pe.wait_ge(constants_made, CONSTANTS)
            every_step(pe, step)


_INS = ["x", "adj", "L0_gnn_W_heads", "L0_gnn_a_heads", "L0_gnn_W_out", "L0_gnn_a_out", "L0_gnn_w1", "L0_gnn_b1",
        "L0_gnn_w2", "L0_gnn_b2", "L0_gnn_ln_gamma", "L0_gnn_ln_beta", "L1_gnn_W", "L1_gnn_a"]


def kernel(**inputs):
    import numpy as np
    import concourse.bacc as bacc
    from concourse import mybir as mb
    from concourse.bass_utils import run_bass_kernel_spmd

    nc = bacc.Bacc("TRN2", target_bir_lowering=False, num_devices=1)
    arrays, args = {}, []
    for name in _INS:
        a = np.ascontiguousarray(inputs[name])
        arrays[f"in_{name}"] = a
        args.append(nc.dram_tensor(f"in_{name}", a.shape, mb.dt.from_np(a.dtype), kind="ExternalInput").ap())
    shape = arrays["in_x"].shape
    args.append(nc.dram_tensor("out_0", shape, mb.dt.float32, kind="ExternalOutput").ap())
    build_gat(nc, *args)
    r = run_bass_kernel_spmd(nc, [arrays], core_ids=[0])
    return r.results[0]["out_0"]
```
